# Optimizing a Trainium2 kernel written in Bass

```python
import numpy as np
import jax
import jax.numpy as jnp

def _softmax(x, axis=-1):
    return jax.nn.softmax(x, axis=axis)

def _gelu(x):
    return jax.nn.gelu(x, approximate=True)

def _silu(x):
    return jax.nn.silu(x)

def _sigmoid(x):
    return jax.nn.sigmoid(x)

def _layernorm(x, axis=-1, eps=1e-05):
    m = jnp.mean(x, axis=axis, keepdims=True)
    v = jnp.var(x, axis=axis, keepdims=True)
    return (x - m) / jnp.sqrt(v + eps)

def _scatter_add(tgt, idx, src, axis=0):
    return tgt.at[idx].add(src)

def _segment_sum(src, seg, n):
    return jax.ops.segment_sum(src, seg, n)
kernel_name = 'mk_cond_resid_d2_seqx_r8_c84dcd'

def setup_inputs(seed: int=0):
    np.random.seed(seed)
    _w = jnp.asarray

    def _rec_inputs():
        import jax
        import jax.numpy as jnp
        _rk = jax.random.key(seed)
        x = 7.22e-05 + 1 * jax.random.normal(jax.random.fold_in(_rk, 1), (8, 128, 512), jnp.float32)
        _lenS = 128 - jax.random.randint(jax.random.fold_in(_rk, 7), (8,), 0, max(1, 128 // 4) + 1, jnp.int32)
        _lenS2 = 128 - jax.random.randint(jax.random.fold_in(_rk, 8), (8,), 0, max(1, 128 // 4) + 1, jnp.int32)
        itok_B_2_6 = jax.random.randint(jax.random.fold_in(_rk, 11), (8,), 2, 7, jnp.int32)
        itok_B_0_2 = jax.random.randint(jax.random.fold_in(_rk, 12), (8,), 0, 3, jnp.int32)
        return (x, itok_B_2_6, itok_B_0_2)
    x, itok_B_2_6, itok_B_0_2 = _rec_inputs()

    def _L0_cond_setup():
        import jax, jax.numpy as jnp
        import numpy as np
        B, N, H, F = (4, 64, 512, 1376)
        L, R, RANK = (1, 16, 16)
        SCALE = 0.5
        key = jax.random.key(seed)
        ks = jax.random.split(key, 12)
        nrm = lambda k, shape, fan: jax.random.normal(k, shape, jnp.float32) * fan ** (-0.5)
        inp = {'x': jax.random.normal(ks[0], (B, N, H), jnp.float32), 'W_gate': nrm(ks[1], (F, H), H), 'W_up': nrm(ks[2], (F, H), H), 'W_down': nrm(ks[3], (H, F), F), 'A_gate': nrm(ks[4], (L, R, RANK, H), H), 'B_gate': nrm(ks[5], (L, R, F, RANK), RANK), 'A_up': nrm(ks[6], (L, R, RANK, H), H), 'B_up': nrm(ks[7], (L, R, F, RANK), RANK), 'A_down': nrm(ks[8], (L, R, RANK, F), F), 'B_down': nrm(ks[9], (L, R, H, RANK), RANK), 'lora_indices': jax.random.randint(ks[10], (B,), 0, R), 'layer_idx': 0}
        return inp
    _L0_cond_all = _L0_cond_setup()
    _L0_cond_in = {k: v for k, v in _L0_cond_all.items() if k in ('W_gate', 'W_up', 'W_down', 'A_gate', 'B_gate', 'A_up', 'B_up', 'A_down', 'B_down')}
    del _L0_cond_all

    def _L1_cond_setup():
        import jax, jax.numpy as jnp
        import numpy as np
        B, S, D_IN, D_OUT = (4, 256, 512, 512)
        R, NUM_LABELERS = (32, 5)
        LORA_SCALING = 16 / 32
        key = jax.random.key(seed)
        k1, k2, k3, k4, k5 = jax.random.split(key, 5)
        x = jax.random.normal(k1, (B, S, D_IN), dtype=jnp.float32)
        labeler_index = jax.random.randint(k2, (B,), 0, NUM_LABELERS, dtype=jnp.int64)
        W = jax.random.normal(k3, (D_OUT, D_IN), dtype=jnp.float32) * 0.02
        lora_A = jax.random.normal(k4, (NUM_LABELERS, D_IN, R), dtype=jnp.float32) * 0.02
        lora_B_w = jax.random.normal(k5, (D_OUT, R), dtype=jnp.float32) * 0.02
        return {'x': x, 'labeler_index': labeler_index, 'W': W, 'lora_A': lora_A, 'lora_B_w': lora_B_w}
    _L1_cond_all = _L1_cond_setup()
    _L1_cond_in = {k: v for k, v in _L1_cond_all.items() if k in ('W', 'lora_A', 'lora_B_w')}
    del _L1_cond_all
    return {'x': x, 'itok_B_2_6': itok_B_2_6, 'itok_B_0_2': itok_B_0_2, 'L0_cond_W_gate': _L0_cond_in['W_gate'], 'L0_cond_W_up': _L0_cond_in['W_up'], 'L0_cond_W_down': _L0_cond_in['W_down'], 'L0_cond_A_gate': _L0_cond_in['A_gate'], 'L0_cond_B_gate': _L0_cond_in['B_gate'], 'L0_cond_A_up': _L0_cond_in['A_up'], 'L0_cond_B_up': _L0_cond_in['B_up'], 'L0_cond_A_down': _L0_cond_in['A_down'], 'L0_cond_B_down': _L0_cond_in['B_down'], 'L1_cond_W': _L1_cond_in['W'], 'L1_cond_lora_A': _L1_cond_in['lora_A'], 'L1_cond_lora_B_w': _L1_cond_in['lora_B_w']}

def reference(x, itok_B_2_6, itok_B_0_2, L0_cond_W_gate, L0_cond_W_up, L0_cond_W_down, L0_cond_A_gate, L0_cond_B_gate, L0_cond_A_up, L0_cond_B_up, L0_cond_A_down, L0_cond_B_down, L1_cond_W, L1_cond_lora_A, L1_cond_lora_B_w):
    import jax
    import jax.numpy as jnp

    def _L0_cond_ref(x, W_gate, W_up, W_down, A_gate, B_gate, A_up, B_up, A_down, B_down, lora_indices, layer_idx):
        import jax, jax.numpy as jnp
        import numpy as np
        B, N, H, F = (4, 64, 512, 1376)
        L, R, RANK = (1, 16, 16)
        SCALE = 0.5

        def lora_add(base, inp, A, B):
            Ab = A[layer_idx][lora_indices]
            Bb = B[layer_idx][lora_indices]
            t = jnp.einsum('bri,bni->bnr', Ab, inp)
            return base + jnp.einsum('bor,bnr->bno', Bb, t) * SCALE
        gate = lora_add(jnp.einsum('bnh,fh->bnf', x, W_gate), x, A_gate, B_gate)
        up = lora_add(jnp.einsum('bnh,fh->bnf', x, W_up), x, A_up, B_up)
        act = jax.nn.silu(gate) * up
        down = lora_add(jnp.einsum('bnf,hf->bnh', act, W_down), act, A_down, B_down)
        return down

    def _L1_cond_ref(x, labeler_index, W, lora_A, lora_B_w):
        import jax, jax.numpy as jnp
        import numpy as np
        B, S, D_IN, D_OUT = (4, 256, 512, 512)
        R, NUM_LABELERS = (32, 5)
        LORA_SCALING = 16 / 32
        base = jnp.einsum('bsi,oi->bso', x, W)
        labelers_A = lora_A[labeler_index]
        low = jnp.einsum('bsi,bir->bsr', x, labelers_A)
        delta = jnp.einsum('bsr,or->bso', low, lora_B_w) * LORA_SCALING
        return base + delta
    x = x + _L0_cond_ref(x, L0_cond_W_gate, L0_cond_W_up, L0_cond_W_down, L0_cond_A_gate, L0_cond_B_gate, L0_cond_A_up, L0_cond_B_up, L0_cond_A_down, L0_cond_B_down, itok_B_2_6, 0)
    x = x + _L1_cond_ref(x, itok_B_0_2, L1_cond_W, L1_cond_lora_A, L1_cond_lora_B_w)
    return x

_drawn_inputs = setup_inputs


def setup_inputs(seed=0):
    import zlib

    import numpy as np

    out = dict(_drawn_inputs(seed))
    spreads = {}
    factors = {}
    for name, (base, spread) in spreads.items():
        noise = np.random.default_rng([zlib.crc32(name.encode()), seed]).standard_normal(out[name].shape)
        drawn = base * np.exp(spread * noise) if base else spread * noise
        out[name] = jnp.asarray(drawn.astype(out[name].dtype))
    for name, factor in factors.items():
        out[name] = (out[name] * factor).astype(out[name].dtype)
    return out
```

```python
from contextlib import ExitStack

import concourse.bass as bass
from concourse import mybir

F32 = mybir.dt.float32
F32R = mybir.dt.float32r
I32 = mybir.dt.int32
ALU = mybir.AluOpType
ACT = mybir.ActivationFunctionType

P = 128
SEQS = 8
TOK = SEQS * P
HALF = 512
HALVES = TOK // HALF
PER_HALF = HALF // P
H = 512
HC = H // P
F = 1376
FC = -(-F // P)
FP = FC * P
RANK = 16
GROUP = 32
STACK = 3 * GROUP
ADAPTERS = 16
LABELERS = 5
LORA_SCALE = 0.5
PIECES = HC
PAIRS = (FC - 1) // 2


def bank_of(c):
    return (6 + 2 * c) % 8


def gated_lora_mlp_then_lora_linear(nc, x_t, adapter, labeler, w_gate_up, w_down, w_one, a_gate_up, a_down, a_one,
                                    b_gate_up, b_down, b_one, out_t):
    with ExitStack() as ctx:
        def sb(name, shape, dt):
            return ctx.enter_context(nc.sbuf_tensor(name, shape, dt))

        def sem(name):
            return ctx.enter_context(nc.semaphore(name))

        x_hi = sb("x_hi", [P, HC, TOK], F32R)
        x_lo = sb("x_lo", [P, HC, TOK], F32R)
        x_full = sb("x_full", [P, HC, TOK], F32)
        act_hi = sb("act_hi", [P, FC, TOK], F32R)
        act_lo = sb("act_lo", [P, FC, TOK], F32R)
        w_raw = sb("w_raw", [P, 2, 2 * H], F32)
        w_hi = sb("w_hi", [P, 2, 2 * H], F32R)
        w_lo = sb("w_lo", [P, 2, 2 * H], F32R)
        b_raw = sb("b_raw", [P, 2, SEQS * 2 * P], F32)
        b_stack = sb("b_stack", [STACK, 2, SEQS * 2 * P], F32R)
        a_late = sb("a_late", [P, FC * SEQS * GROUP], F32R)
        t_stack = sb("t_stack", [STACK, TOK], F32R)
        idx_raw = sb("idx_raw", [1, 2, SEQS], I32)
        idx_wrap = sb("idx_wrap", [1, 2, SEQS], I32)
        idx_sum = sb("idx_sum", [1, 2, SEQS], I32)
        idx = sb("idx", [1, 2, SEQS], I32)
        psum = ctx.enter_context(nc.psum_tensor("psum", [P, 8, HALF], F32))

        silu = x_full[:, HC - 1, :]
        a_gu_raw = x_full[:, 0, :]
        a_down_raw = x_full[:, 1:3, :].rearrange("p a b -> p (a b)")[:, 0:SEQS * FC * RANK]
        a_gu_hi = act_hi[:, FC - 1, :].rearrange("p (k c) -> p k c", k=HC)
        a_gu_lo = act_lo[:, FC - 1, :].rearrange("p (k c) -> p k c", k=HC)
        a_down_hl = a_late[:, :].rearrange("p (f b c) -> p f b c", f=FC, b=SEQS)
        A1 = HC * SEQS * GROUP
        a_one_hi = a_late[:, 0:A1].rearrange("p (k c) -> p k c", k=HC)
        a_one_lo = a_late[:, A1:2 * A1].rearrange("p (k c) -> p k c", k=HC)
        b_one_stack = a_late[0:STACK, 2 * A1:2 * A1 + H]
        b_down_raw = b_raw[0:STACK, :, :].rearrange("p a (b c) -> p (a b) c", c=H)
        b_down_stack = b_stack[:, :, :].rearrange("p a (b c) -> p (a b) c", c=H)
        a_one_raw = b_raw[:, 0, 0:A1]
        b_one_raw = b_raw[0:STACK, 1, 0:H]

        x_loaded = [sem(f"x_loaded{k}") for k in range(HC)]
        w0_loaded = [sem(f"w0_loaded{k}") for k in range(HC)]
        w_loaded = [sem(f"w_loaded{s}") for s in range(2)]
        down_loaded = [sem(f"down_loaded{s}") for s in range(2)]
        one_loaded = [sem(f"one_loaded{k}") for k in range(HC)]
        idx_loaded = sem("idx_loaded")
        a_gu_loaded = sem("a_gu_loaded")
        a_down_loaded = sem("a_down_loaded")
        a_one_loaded = sem("a_one_loaded")
        b_loaded = [sem(f"b_loaded{s}") for s in range(2)]
        b_down_loaded = sem("b_down_loaded")
        b_one_loaded = sem("b_one_loaded")
        idx_step = sem("idx_step")
        x_hi_ready = sem("x_hi_ready")
        x_lo_ready = sem("x_lo_ready")
        x_full_ready = sem("x_full_ready")
        w_hi_ready = sem("w_hi_ready")
        w_lo_ready = sem("w_lo_ready")
        down_hi_ready = sem("down_hi_ready")
        down_lo_ready = sem("down_lo_ready")
        one_hi_ready = sem("one_hi_ready")
        one_lo_ready = sem("one_lo_ready")
        a_gu_hi_ready = sem("a_gu_hi_ready")
        a_gu_lo_ready = sem("a_gu_lo_ready")
        a_down_hi_ready = sem("a_down_hi_ready")
        a_down_lo_ready = sem("a_down_lo_ready")
        a_one_hi_ready = sem("a_one_hi_ready")
        a_one_lo_ready = sem("a_one_lo_ready")
        b_hi_ready = sem("b_hi_ready")
        b_ready = sem("b_ready")
        b_down_hi_ready = sem("b_down_hi_ready")
        b_down_ready = sem("b_down_ready")
        b_one_hi_ready = sem("b_one_hi_ready")
        b_one_ready = sem("b_one_ready")
        t_done = sem("t_done")
        t_hi_ready = sem("t_hi_ready")
        t_again_ready = sem("t_again_ready")
        t_lo_ready = sem("t_lo_ready")
        gate_done = sem("gate_done")
        gate_up_done = sem("gate_up_done")
        silu_done = sem("silu_done")
        mult_done = sem("mult_done")
        act_hi_ready = sem("act_hi_ready")
        act_lo_ready = sem("act_lo_ready")
        down_step_done = sem("down_step_done")
        down_done = sem("down_done")
        x1_ready = sem("x1_ready")
        x1_hi_ready = sem("x1_hi_ready")
        x1_lo_ready = sem("x1_lo_ready")
        out_done = sem("out_done")
        out_ready = sem("out_ready")
        stored = sem("stored")

        block = ctx.enter_context(nc.Block())

        def gate_banks(s):
            return psum[:, 4 * s:4 * s + 2, :]

        def up_banks(s):
            return psum[:, 4 * s + 2:4 * s + 4, :]

        @block.sync
        def _(sp):
            def load_gate_up(f, slot):
                sp.dma_start(w_raw[:, slot, :], w_gate_up[bass.ds(f, 1), :, :].rearrange("a p n -> (a p) n")).then_inc(w_loaded[slot], 16)

            def load_b(f, slot, seq):
                for b in range(SEQS):
                    sp.dma_start(b_raw[0:STACK, slot, b * 2 * P:(b + 1) * 2 * P],
                                 b_gate_up[bass.ds(seq[b], 1), bass.ds(f, 1), :, :].rearrange("i f p n -> (i f p) n")
                                 ).then_inc(b_loaded[slot], 16)

            def load_down(f, slot):
                sp.dma_start(w_raw[:, 1, slot * H:(slot + 1) * H],
                             w_down[bass.ds(f, 1), :, :].rearrange("a p n -> (a p) n")).then_inc(down_loaded[slot], 16)

            def load_one(k, slot, half):
                sp.dma_start(w_raw[:, slot, half * H:(half + 1) * H], w_one[k * P:(k + 1) * P, :]).then_inc(one_loaded[k], 16)

            sp.dma_start(idx_raw[:, 0, :], adapter).then_inc(idx_loaded, 16)
            sp.dma_start(idx_raw[:, 1, :], labeler).then_inc(idx_loaded, 16)
            piece = 2 * H // PIECES
            for k in range(HC):
                sp.dma_start(w_raw[:, 0, k * piece:(k + 1) * piece],
                             w_gate_up[0, :, k * piece:(k + 1) * piece]).then_inc(w0_loaded[k], 16)
                sp.dma_start(x_full[:, k, :], x_t[k * P:(k + 1) * P, :]).then_inc(x_loaded[k], 16)
            sp.wait_ge(idx_step, 3)
            seq = [sp.value_load(idx[0:1, 0, b:b + 1], min_val=0, max_val=ADAPTERS - 1) for b in range(SEQS)]
            sp.wait_ge(x_lo_ready, 1)
            for b in range(SEQS):
                sp.dma_start(a_gu_raw[:, b * P:(b + 1) * P],
                             a_gate_up[bass.ds(seq[b], 1), :, :].rearrange("i p n -> (i p) n")).then_inc(a_gu_loaded, 16)
            load_b(0, 0, seq)
            load_gate_up(1, 1)
            load_b(1, 1, seq)
            sp.wait_ge(x_lo_ready, 3)
            for b in range(SEQS):
                sp.dma_start(a_down_raw[:, b * FC * RANK:(b + 1) * FC * RANK],
                             a_down[bass.ds(seq[b], 1), :, :].rearrange("i p n -> (i p) n")).then_inc(a_down_loaded, 16)

            def load_step(f, slot):
                sp.wait_ge(w_lo_ready, f + PIECES - 2)
                load_gate_up(f, slot)
                sp.wait_ge(b_ready, f - 1)
                load_b(f, slot, seq)

            with sp.Fori(1, PAIRS) as pair:
                load_step(2 * pair, 0)
                load_step(2 * pair + 1, 1)
            load_step(FC - 1, 0)

            for f in range(2):
                if f == 0:
                    sp.wait_ge(w_lo_ready, PIECES + FC - 2)
                load_down(f, f)
            sp.wait_ge(w_lo_ready, PIECES + FC - 1)
            load_one(0, 0, 0)
            load_one(1, 0, 1)
            sp.wait_ge(b_ready, FC)
            for b in range(SEQS):
                sp.dma_start(b_down_raw[:, b, :],
                             b_down[bass.ds(seq[b], 1), :, :].rearrange("i p n -> (i p) n")).then_inc(b_down_loaded, 16)
            for f in (2, 3):
                sp.wait_ge(down_lo_ready, f - 1)
                load_down(f, f % 2)
            label = [sp.value_load(idx[0:1, 1, b:b + 1], min_val=0, max_val=LABELERS - 1) for b in range(SEQS)]
            sp.wait_ge(b_down_ready, 1)
            for b in range(SEQS):
                sp.dma_start(a_one_raw[:, b * P:(b + 1) * P],
                             a_one[bass.ds(label[b], 1), :, :].rearrange("i p n -> (i p) n")).then_inc(a_one_loaded, 16)
            sp.dma_start(b_one_raw, b_one).then_inc(b_one_loaded, 16)
            with sp.Fori(2, PAIRS) as pair:
                for s in range(2):
                    sp.wait_ge(down_lo_ready, 2 * pair + s - 1)
                    load_down(2 * pair + s, s)
            sp.wait_ge(down_lo_ready, FC - 2)
            load_down(FC - 1, 0)
            sp.wait_ge(down_lo_ready, FC - 1)
            load_one(2, 1, 1)
            sp.wait_ge(down_lo_ready, FC)
            load_one(3, 1, 0)

            for o in range(HC):
                for n in range(HALVES):
                    sp.wait_ge(out_ready, HALVES * o + n + 1)
                    sp.dma_start(out_t[o * P:(o + 1) * P, n * HALF:(n + 1) * HALF],
                                 x_full[:, o, n * HALF:(n + 1) * HALF]).then_inc(stored, 16)
            sp.wait_ge(stored, 16 * HC * HALVES)

        @block.gpsimd
        def _(pool):
            def b_lo(f, slot):
                pool.wait_ge(b_hi_ready, f + 1)
                last = b_stack[2 * GROUP:STACK, slot, :]
                nc.gpsimd.tensor_tensor(last, b_raw[2 * GROUP:STACK, slot, :], last.bitcast(F32), ALU.subtract).then_inc(b_ready, 1)

            with pool.Fori(0, PAIRS) as pair:
                b_lo(2 * pair, 0)
                b_lo(2 * pair + 1, 1)
            b_lo(FC - 1, 0)

            pool.wait_ge(b_down_hi_ready, 1)
            last = b_down_stack[2 * GROUP:STACK, :, :]
            nc.gpsimd.tensor_tensor(last, b_down_raw[2 * GROUP:STACK, :, :], last.bitcast(F32), ALU.subtract).then_inc(b_down_ready, 1)
            pool.wait_ge(b_down_ready, 1)
            pool.wait_ge(a_gu_lo_ready, 1)
            pool.wait_ge(a_down_lo_ready, 1)
            pool.wait_ge(mult_done, FC)
            for k in range(HC):
                nc.gpsimd.tensor_tensor(x_full[:, k, :], x_hi[:, k, :].bitcast(F32), x_lo[:, k, :].bitcast(F32),
                                        ALU.add).then_inc(x_full_ready, 1)
            pool.wait_ge(x_full_ready, HC)
            pool.wait_ge(b_one_hi_ready, 1)
            last = b_one_stack[2 * GROUP:STACK, :]
            nc.gpsimd.tensor_tensor(last, b_one_raw[2 * GROUP:STACK, :], last.bitcast(F32), ALU.subtract).then_inc(b_one_ready, 1)

        def sequences_of_quadrant(banks, j):
            return banks[GROUP * j:GROUP * (j + 1), :, j * P:(j + 1) * P]

        def in_stack(part, j):
            rows = t_stack[GROUP * part:GROUP * (part + 1), :].rearrange("p (n c) -> p n c", n=HALVES)
            return rows[:, :, j * P:(j + 1) * P]

        t_banks = psum[:, bank_of(HC - 1):bank_of(HC - 1) + 2, :]

        @block.scalar
        def _(act):
            piece = 2 * H // PIECES

            def hi_of_weights(loads, f, slot):
                act.wait_ge(w_loaded[slot], loads)
                nc.scalar.copy(w_hi[:, slot, :], w_raw[:, slot, :]).then_inc(w_hi_ready, 1)

            def hi_of_b(pair, slot):
                act.wait_ge(b_loaded[slot], 16 * SEQS * (pair + 1))
                nc.scalar.copy(b_stack[:, slot, :], b_raw[0:STACK, slot, :]).then_inc(b_hi_ready, 1)

            def hi_of_tile(hi, raw, ready):
                nc.scalar.copy(hi, raw).then_inc(ready, 1)

            def hi_of_t(use):
                act.wait_ge(t_done, use + 1)
                for j in range(PER_HALF):
                    nc.scalar.activation(in_stack(0, j), sequences_of_quadrant(t_banks, j), ACT.Copy,
                                         scale=LORA_SCALE).then_inc(t_hi_ready, 1)
                act.wait_ge(t_hi_ready, PER_HALF * (use + 1))
                nc.scalar.copy(t_stack[2 * GROUP:STACK, :], t_stack[0:GROUP, :].bitcast(F32)).then_inc(t_again_ready, 1)

            def activate(f, s):
                act.wait_ge(gate_done, f + 1)
                nc.scalar.activation(silu, gate_banks(s).rearrange("p n c -> p (n c)"), ACT.Silu).then_inc(silu_done, 1)

            def hi_of_act(f, s):
                act.wait_ge(mult_done, f + 1)
                nc.scalar.copy(act_hi[:, bass.ds(f, 1), :].rearrange("p a n -> p (a n)"),
                               up_banks(s).rearrange("p n c -> p (n c)")).then_inc(act_hi_ready, 1)

            for k in range(HC):
                act.wait_ge(w0_loaded[k], 16)
                cols = slice(k * piece, (k + 1) * piece)
                nc.scalar.copy(w_hi[:, 0, cols], w_raw[:, 0, cols]).then_inc(w_hi_ready, 1)
                act.wait_ge(x_loaded[k], 16)
                nc.scalar.copy(x_hi[:, k, :], x_full[:, k, :]).then_inc(x_hi_ready, 1)
            act.wait_ge(a_gu_loaded, 16 * SEQS)
            nc.scalar.copy(a_gu_hi.rearrange("p k (b c) -> p k b c", b=SEQS),
                           a_gu_raw.rearrange("p (b k c) -> p k b c", b=SEQS, k=HC)).then_inc(a_gu_hi_ready, 1)
            hi_of_b(0, 0)
            hi_of_weights(16, 1, 1)
            hi_of_t(0)
            hi_of_b(0, 1)
            act.wait_ge(a_down_loaded, 16 * SEQS)
            nc.scalar.copy(a_down_hl[:, :, :, 0:RANK],
                           a_down_raw.rearrange("p (b f c) -> p f b c", b=SEQS, f=FC)).then_inc(a_down_hi_ready, 1)
            activate(0, 0)
            hi_of_act(0, 0)

            def step(f, s, pair_of_next):
                act.wait_ge(gate_up_done, f)
                hi_of_weights(16 * (pair_of_next + (1 if s == 0 else 0)), f + 1, 1 - s)
                hi_of_b(pair_of_next, 1 - s)
                act.wait_ge(mult_done, f)
                activate(f, s)
                hi_of_act(f, s)

            with act.Fori(0, PAIRS - 1) as pair:
                step(2 * pair + 1, 1, pair + 1)
                step(2 * pair + 2, 0, pair + 1)
            step(FC - 2, 1, PAIRS)

            def hi_of_down(f, loads, slot):
                act.wait_ge(down_loaded[slot], loads)
                cols = slice(slot * H, (slot + 1) * H)
                nc.scalar.copy(w_hi[:, 1, cols], w_raw[:, 1, cols]).then_inc(down_hi_ready, 1)

            def hi_of_one(k, slot, half):
                act.wait_ge(one_loaded[k], 16)
                cols = slice(half * H, (half + 1) * H)
                nc.scalar.copy(w_hi[:, slot, cols], w_raw[:, slot, cols]).then_inc(one_hi_ready, 1)

            act.wait_ge(gate_up_done, FC - 1)
            hi_of_down(0, 16, 0)
            hi_of_down(1, 16, 1)
            act.wait_ge(mult_done, FC - 1)
            activate(FC - 1, 0)
            hi_of_act(FC - 1, 0)
            act.wait_ge(gate_up_done, FC)
            act.wait_ge(b_down_loaded, 16 * SEQS)
            nc.scalar.copy(b_down_stack, b_down_raw).then_inc(b_down_hi_ready, 1)
            hi_of_one(0, 0, 0)
            hi_of_one(1, 0, 1)
            hi_of_t(1)
            with act.Fori(1, PAIRS) as pair:
                for s in range(2):
                    act.wait_ge(down_step_done, 2 * pair + s - 1)
                    hi_of_down(2 * pair + s, 16 * (pair + 1), s)
            act.wait_ge(down_step_done, FC - 2)
            hi_of_down(FC - 1, 16 * (PAIRS + 1), 0)
            act.wait_ge(a_one_loaded, 16 * SEQS)
            nc.scalar.copy(a_one_hi.rearrange("p k (b c) -> p k b c", b=SEQS),
                           a_one_raw.rearrange("p (b k c) -> p k b c", b=SEQS, k=HC)).then_inc(a_one_hi_ready, 1)
            act.wait_ge(b_one_loaded, 16)
            nc.scalar.copy(b_one_stack, b_one_raw).then_inc(b_one_hi_ready, 1)
            act.wait_ge(down_step_done, FC - 1)
            hi_of_one(2, 1, 1)
            for c in range(HC):
                act.wait_ge(x1_ready, c + 1)
                nc.scalar.copy(x_hi[:, c, :], x_full[:, c, :]).then_inc(x1_hi_ready, 1)
            act.wait_ge(down_done, HC)
            hi_of_one(3, 1, 0)
            hi_of_t(2)

        @block.vector
        def _(dve):
            piece = 2 * H // PIECES

            def lo(out, raw, hi, ready):
                nc.vector.tensor_tensor(out, raw, hi.bitcast(F32), ALU.subtract).then_inc(ready, 1)

            def lo_of_weights(f, slot):
                dve.wait_ge(w_hi_ready, f + PIECES)
                lo(w_lo[:, slot, :], w_raw[:, slot, :], w_hi[:, slot, :], w_lo_ready)

            def lo_of_t(use):
                for j in range(PER_HALF):
                    dve.wait_ge(t_hi_ready, PER_HALF * use + j + 1)
                    nc.vector.scalar_tensor_tensor(in_stack(1, j), sequences_of_quadrant(t_banks, j), LORA_SCALE,
                                                   in_stack(0, j).bitcast(F32), ALU.mult, ALU.subtract
                                                   ).then_inc(t_lo_ready, 1)

            def multiply(f, s):
                dve.wait_ge(silu_done, f + 1)
                dve.wait_ge(gate_up_done, f + 1)
                up = up_banks(s).rearrange("p n c -> p (n c)")
                nc.vector.tensor_tensor(up, silu, up, ALU.mult).then_inc(mult_done, 1)

            def lo_of_act(f, s):
                dve.wait_ge(act_hi_ready, f + 1)
                at = bass.ds(f, 1)
                nc.vector.tensor_tensor(act_lo[:, at, :].rearrange("p a n -> p (a n)"),
                                        up_banks(s).rearrange("p n c -> p (n c)"),
                                        act_hi[:, at, :].rearrange("p a n -> p (a n)").bitcast(F32),
                                        ALU.subtract).then_inc(act_lo_ready, 1)

            dve.wait_ge(idx_loaded, 32)
            for t, n in ((0, ADAPTERS), (1, LABELERS)):
                last = nc.vector.tensor_scalar(idx_wrap[:, t, :], idx_raw[:, t, :], 0, n, ALU.is_lt, ALU.mult)
            last.then_inc(idx_step, 1)
            dve.wait_ge(idx_step, 1)
            nc.vector.tensor_tensor(idx_sum[:, :, :], idx_raw[:, :, :], idx_wrap[:, :, :], ALU.add).then_inc(idx_step, 1)
            dve.wait_ge(idx_step, 2)
            for t, n in ((0, ADAPTERS), (1, LABELERS)):
                last = nc.vector.tensor_scalar(idx[:, t, :], idx_sum[:, t, :], 0, n - 1, ALU.max, ALU.min)
            last.then_inc(idx_step, 1)

            for k in range(HC):
                dve.wait_ge(w_hi_ready, k + 1)
                cols = slice(k * piece, (k + 1) * piece)
                lo(w_lo[:, 0, cols], w_raw[:, 0, cols], w_hi[:, 0, cols], w_lo_ready)
                dve.wait_ge(x_hi_ready, k + 1)
                lo(x_lo[:, k, :], x_full[:, k, :], x_hi[:, k, :], x_lo_ready)
            dve.wait_ge(a_gu_hi_ready, 1)
            lo(a_gu_lo.rearrange("p k (b c) -> p k b c", b=SEQS), a_gu_raw.rearrange("p (b k c) -> p k b c", b=SEQS, k=HC),
               a_gu_hi.rearrange("p k (b c) -> p k b c", b=SEQS), a_gu_lo_ready)
            lo_of_weights(1, 1)
            lo_of_t(0)
            dve.wait_ge(a_down_hi_ready, 1)
            lo(a_down_hl[:, :, :, RANK:GROUP], a_down_raw.rearrange("p (b f c) -> p f b c", b=SEQS, f=FC),
               a_down_hl[:, :, :, 0:RANK], a_down_lo_ready)
            multiply(0, 0)
            lo_of_act(0, 0)

            def step(f, s):
                lo_of_weights(f + 1, 1 - s)
                multiply(f, s)
                lo_of_act(f, s)

            with dve.Fori(0, PAIRS - 1) as pair:
                step(2 * pair + 1, 1)
                step(2 * pair + 2, 0)
            step(FC - 2, 1)

            def lo_of_down(f, slot):
                dve.wait_ge(down_hi_ready, f + 1)
                cols = slice(slot * H, (slot + 1) * H)
                lo(w_lo[:, 1, cols], w_raw[:, 1, cols], w_hi[:, 1, cols], down_lo_ready)

            def lo_of_one(k, slot, half):
                dve.wait_ge(one_hi_ready, k + 1)
                cols = slice(half * H, (half + 1) * H)
                lo(w_lo[:, slot, cols], w_raw[:, slot, cols], w_hi[:, slot, cols], one_lo_ready)

            lo_of_down(0, 0)
            lo_of_down(1, 1)
            multiply(FC - 1, 0)
            lo_of_act(FC - 1, 0)
            lo_of_one(0, 0, 0)
            lo_of_one(1, 0, 1)
            lo_of_t(1)
            with dve.Fori(1, PAIRS) as pair:
                lo_of_down(2 * pair, 0)
                lo_of_down(2 * pair + 1, 1)
            lo_of_down(FC - 1, 0)
            dve.wait_ge(a_one_hi_ready, 1)
            lo(a_one_lo.rearrange("p k (b c) -> p k b c", b=SEQS), a_one_raw.rearrange("p (b k c) -> p k b c", b=SEQS, k=HC),
               a_one_hi.rearrange("p k (b c) -> p k b c", b=SEQS), a_one_lo_ready)
            lo_of_one(2, 1, 1)
            for c in range(HC):
                dve.wait_ge(down_done, c + 1)
                dve.wait_ge(x_full_ready, c + 1)
                at = psum[:, bank_of(c):bank_of(c) + 2, :].rearrange("p n c -> p (n c)")
                nc.vector.tensor_tensor(x_full[:, c, :], at, x_full[:, c, :], ALU.add).then_inc(x1_ready, 1)
                dve.wait_ge(x1_hi_ready, c + 1)
                lo(x_lo[:, c, :], x_full[:, c, :], x_hi[:, c, :], x1_lo_ready)
            lo_of_one(3, 1, 0)
            lo_of_t(2)
            for o in range(HC):
                dve.wait_ge(out_done, o + 1)
                for n in range(HALVES):
                    cols = slice(n * HALF, (n + 1) * HALF)
                    nc.vector.tensor_tensor(x_full[:, o, cols], psum[:, bank_of(o) + n, :], x_full[:, o, cols],
                                            ALU.add).then_inc(out_ready, 1)

        @block.tensor
        def _(pe):
            def product(out, w_parts, v_parts, first):
                (w_h, w_l), (v_h, v_l) = w_parts, v_parts
                for w, v in ((w_h, v_h), (w_h, v_l), (w_l, v_h)):
                    for n in range(HALVES):
                        mm = nc.tensor.matmul(out[:, n, :], w, v[:, n * HALF:(n + 1) * HALF],
                                              start=first and w is w_h and v is v_h, stop=False)
                return mm

            def t_product(a_h, a_l, v_h, v_l, k, first, last):
                for n in range(HALVES):
                    cols = slice(n * P, (n + 1) * P)
                    tok = slice(n * HALF, (n + 1) * HALF)
                    for w, v in ((a_h, v_h), (a_h, v_l), (a_l, v_h)):
                        mm = nc.tensor.matmul(t_banks[:, n, :], w[:, k, cols], v[:, k, tok],
                                              start=first and w is a_h and v is v_h, stop=last and w is a_l)
                return mm

            def adapters(out, stack_of):
                for b in range(SEQS):
                    n, j = divmod(b, PER_HALF)
                    mm = nc.tensor.matmul(out[:, n, j * P:(j + 1) * P], stack_of(b), t_stack[:, b * P:(b + 1) * P],
                                          start=False, stop=j == PER_HALF - 1)
                return mm

            def gate_up_chunk(k, s):
                for g, out in enumerate((gate_banks(s), up_banks(s))):
                    cols = slice((2 * k + g) * P, (2 * k + g + 1) * P)
                    product(out, (w_hi[:, s, cols], w_lo[:, s, cols]), (x_hi[:, k, :], x_lo[:, k, :]), k == 0)

            def gate_up_adapters(f, s):
                pe.wait_ge(b_ready, f + 1)
                for g, (out, done) in enumerate(((gate_banks(s), gate_done), (up_banks(s), gate_up_done))):
                    adapters(out, lambda b, g=g: b_stack[:, s, (2 * b + g) * P:(2 * b + g + 1) * P]).then_inc(done, 1)

            def step(f, s, reused=True):
                pe.wait_ge(w_hi_ready, f + PIECES)
                pe.wait_ge(w_lo_ready, f + PIECES)
                if reused:
                    pe.wait_ge(silu_done, f - 1)
                    pe.wait_ge(act_lo_ready, f - 1)
                for k in range(HC):
                    gate_up_chunk(k, s)
                gate_up_adapters(f, s)

            for k in range(HC):
                if k == HC - 1:
                    pe.wait_ge(x_hi_ready, HC)
                    pe.wait_ge(x_lo_ready, HC)
                    pe.wait_ge(a_gu_hi_ready, 1)
                    pe.wait_ge(a_gu_lo_ready, 1)
                    for kk in range(HC):
                        mm = t_product(a_gu_hi, a_gu_lo, x_hi, x_lo, kk, kk == 0, kk == HC - 1)
                    mm.then_inc(t_done, 1)
                pe.wait_ge(w_hi_ready, k + 1)
                pe.wait_ge(w_lo_ready, k + 1)
                pe.wait_ge(x_hi_ready, k + 1)
                pe.wait_ge(x_lo_ready, k + 1)
                gate_up_chunk(k, 0)
            pe.wait_ge(t_again_ready, 1)
            pe.wait_ge(t_lo_ready, PER_HALF)
            gate_up_adapters(0, 0)
            step(1, 1, reused=False)
            with pe.Fori(1, PAIRS) as pair:
                step(2 * pair, 0)
                step(2 * pair + 1, 1)
            step(FC - 1, 0)

            pe.wait_ge(a_down_lo_ready, 1)
            pe.wait_ge(act_lo_ready, FC - 1)
            for f in range(FC):
                if f == FC - 1:
                    pe.wait_ge(act_lo_ready, FC)
                for n in range(HALVES):
                    for v in (act_hi, act_lo):
                        mm = nc.tensor.matmul(t_banks[:, n, :],
                                              a_down_hl[:, f, n * PER_HALF:(n + 1) * PER_HALF, :].rearrange("p b c -> p (b c)"),
                                              v[:, f, n * HALF:(n + 1) * HALF],
                                              start=f == 0 and v is act_hi, stop=f == FC - 1 and v is act_lo)
            mm.then_inc(t_done, 1)

            def banks(c):
                return psum[:, bank_of(c):bank_of(c) + 2, :]

            def down_chunk(f, slot, c, first=False):
                cols = slice(slot * H + c * P, slot * H + (c + 1) * P)
                at = bass.ds(f, 1)
                return product(banks(c), (w_hi[:, 1, cols], w_lo[:, 1, cols]),
                               (act_hi[:, at, :].rearrange("p a n -> p (a n)"), act_lo[:, at, :].rearrange("p a n -> p (a n)")), first)

            def down_step(f, slot, first=False):
                pe.wait_ge(down_hi_ready, f + 1)
                pe.wait_ge(down_lo_ready, f + 1)
                for c in range(HC):
                    if first and c == HC - 1:
                        pe.wait_ge(t_hi_ready, 2 * PER_HALF)
                        pe.wait_ge(t_lo_ready, 2 * PER_HALF)
                    mm = down_chunk(f, slot, c, first)
                mm.then_inc(down_step_done, 1)

            down_step(0, 0, first=True)
            down_step(1, 1)
            with pe.Fori(1, PAIRS) as pair:
                down_step(2 * pair, 0)
                down_step(2 * pair + 1, 1)
            pe.wait_ge(down_hi_ready, FC)
            pe.wait_ge(down_lo_ready, FC)
            pe.wait_ge(t_again_ready, 2)
            pe.wait_ge(b_down_ready, 1)
            for c in range(HC):
                down_chunk(FC - 1, 0, c)
                adapters(banks(c), lambda b: b_down_stack[:, b, c * P:(c + 1) * P]).then_inc(down_done, 1)

            place = [(0, 0), (0, 1), (1, 1), (1, 0)]

            def one_chunk(k, o):
                slot, half = place[k]
                cols = slice(half * H + o * P, half * H + (o + 1) * P)
                product(banks(o), (w_hi[:, slot, cols], w_lo[:, slot, cols]), (x_hi[:, k, :], x_lo[:, k, :]), k == 0)

            pe.wait_ge(a_one_hi_ready, 1)
            pe.wait_ge(a_one_lo_ready, 1)
            for k in range(HC):
                pe.wait_ge(one_hi_ready, k + 1)
                pe.wait_ge(one_lo_ready, k + 1)
                pe.wait_ge(x1_hi_ready, k + 1)
                pe.wait_ge(x1_lo_ready, k + 1)
                if k == HC - 1:
                    t_product(a_one_hi, a_one_lo, x_hi, x_lo, k, False, True).then_inc(t_done, 1)
                for o in range(HC - 1):
                    if k == 0:
                        pe.wait_ge(x1_ready, o + 1)
                    one_chunk(k, o)
                if k == 0:
                    pe.wait_ge(x1_ready, HC)
                if k < HC - 1:
                    t_product(a_one_hi, a_one_lo, x_hi, x_lo, k, k == 0, False)
            pe.wait_ge(b_one_ready, 1)
            pe.wait_ge(t_lo_ready, 3 * PER_HALF)
            pe.wait_ge(t_again_ready, 3)
            for o in range(HC):
                if o == HC - 1:
                    for k in range(HC):
                        one_chunk(k, o)
                for n in range(HALVES):
                    mm = nc.tensor.matmul(banks(o)[:, n, :], b_one_stack[:, o * P:(o + 1) * P],
                                          t_stack[:, n * HALF:(n + 1) * HALF], start=False, stop=True)
                mm.then_inc(out_done, 1)


def kernel(x, itok_B_2_6, itok_B_0_2, L0_cond_W_gate, L0_cond_W_up, L0_cond_W_down, L0_cond_A_gate, L0_cond_B_gate,
           L0_cond_A_up, L0_cond_B_up, L0_cond_A_down, L0_cond_B_down, L1_cond_W, L1_cond_lora_A, L1_cond_lora_B_w):
    import numpy as np
    import concourse.bacc as bacc
    from concourse.bass_utils import run_bass_kernel_spmd

    def padded(a, axis):
        pad = [(0, 0)] * a.ndim
        pad[axis] = (0, FP - F)
        return np.pad(a, pad)

    gate_up = np.stack([padded(np.asarray(w), 0).reshape(FC, P, HC, P) for w in (L0_cond_W_gate, L0_cond_W_up)])
    gate_up = gate_up.transpose(1, 4, 3, 0, 2).reshape(FC, P, 2 * H)
    down = padded(np.asarray(L0_cond_W_down), 1).T.reshape(FC, P, H)
    one = np.asarray(L1_cond_W).T
    a_gate_up = np.concatenate([np.asarray(L0_cond_A_gate)[0], np.asarray(L0_cond_A_up)[0]], 1)
    a_gate_up = a_gate_up.reshape(ADAPTERS, GROUP, HC, P).transpose(0, 3, 2, 1).reshape(ADAPTERS, P, HC * GROUP)
    a_down = padded(np.asarray(L0_cond_A_down)[0], 2).reshape(ADAPTERS, RANK, FC, P).transpose(0, 3, 2, 1)
    a_down = a_down.reshape(ADAPTERS, P, FC * RANK)
    a_one = np.asarray(L1_cond_lora_A).reshape(LABELERS, HC, P, GROUP).transpose(0, 2, 1, 3).reshape(LABELERS, P, HC * GROUP)
    b_gate_up = np.zeros((ADAPTERS, FC, 3, 2, RANK, 2, P), np.float32)
    for g, b in enumerate((L0_cond_B_gate, L0_cond_B_up)):
        b = padded(np.asarray(b)[0], 1).reshape(ADAPTERS, FC, P, RANK).transpose(0, 1, 3, 2)
        b_gate_up[:, :, :, g, :, g, :] = b[:, :, None]
    b_gate_up = b_gate_up.reshape(ADAPTERS, FC, STACK, 2 * P)
    b_down = np.tile(np.asarray(L0_cond_B_down)[0].transpose(0, 2, 1), (1, STACK // RANK, 1))
    b_one = np.tile(np.asarray(L1_cond_lora_B_w).T, (3, 1))

    nc = bacc.Bacc("TRN2", target_bir_lowering=False, num_devices=1)
    host = {
        "x_t": np.asarray(x).reshape(TOK, H).T,
        "adapter": np.asarray(itok_B_2_6).reshape(1, SEQS),
        "labeler": np.asarray(itok_B_0_2).reshape(1, SEQS),
        "w_gate_up": gate_up, "w_down": down, "w_one": one,
        "a_gate_up": a_gate_up, "a_down": a_down, "a_one": a_one,
        "b_gate_up": b_gate_up, "b_down": b_down, "b_one": b_one,
    }
    host = {name: np.ascontiguousarray(a) for name, a in host.items()}
    aps = [nc.dram_tensor(name, a.shape, mybir.dt.from_np(a.dtype), kind="ExternalInput").ap() for name, a in host.items()]
    out_t = nc.dram_tensor("out_t", (H, TOK), F32, kind="ExternalOutput").ap()
    gated_lora_mlp_then_lora_linear(nc, *aps, out_t)
    result = run_bass_kernel_spmd(nc, [host], core_ids=[0])
    return result.results[0]["out_t"].T.reshape(SEQS, P, H)
```

```python
from contextlib import ExitStack

import concourse.bass as bass
from concourse import mybir
from concourse.bass import OrderedEngineSet

F32 = mybir.dt.float32
F32R = mybir.dt.float32r
I32 = mybir.dt.int32
ALU = mybir.AluOpType
ACT = mybir.ActivationFunctionType

P = 128
SEQS = 8
TOK = SEQS * P
HALF = 512
HALVES = TOK // HALF
PER_HALF = HALF // P
H = 512
HC = H // P
F = 1376
FC = -(-F // P)
SHORT = F - (FC - 1) * P
RANK = 16
GROUP = 32
PAIR = 2 * P
PAIRS_OF_SEQS = SEQS // 2
STACK = 3 * GROUP
ADAPTERS = 16
LABELERS = 5
LORA_SCALE = 0.5
X_PIECES = HC + 1
PIECES = HC
PAIRS = (FC - 1) // 2
WARM_UP = 8


def bank_of(c):
    return (6 + 2 * c) % 8


def gated_lora_mlp_then_lora_linear(nc, x_t, sequence_indices, own, w_gate_up, w_down, w_one, a_gate_up, a_down, a_one,
                                    b_gate_up, b_down, b_one, out_t):
    with ExitStack() as ctx:
        def sb(name, shape, dt):
            return ctx.enter_context(nc.sbuf_tensor(name, shape, dt))

        def sem(name):
            return ctx.enter_context(nc.semaphore(name))

        x_hi = sb("x_hi", [P, HC, TOK], F32R)
        x_lo = sb("x_lo", [P, HC, TOK], F32R)
        x_full = sb("x_full", [P, HC, TOK], F32)
        act_hi = sb("act_hi", [P, FC, TOK], F32R)
        act_lo = sb("act_lo", [P, FC, TOK], F32R)
        w_raw = sb("w_raw", [P, 2, 2 * H], F32)
        w_hi = sb("w_hi", [P, 2, 2 * H], F32R)
        w_lo = sb("w_lo", [P, 2, 2 * H], F32R)
        b_raw = sb("b_raw", [P, 2, PAIRS_OF_SEQS * 2 * P], F32)
        b_stack = sb("b_stack", [STACK, 2, PAIRS_OF_SEQS * 2 * P], F32R)
        a_late = sb("a_late", [P, FC * SEQS * GROUP], F32R)
        t_stacks = [sb(f"t_stack{g}", [STACK, TOK], F32R) for g in range(2)]
        t_stack = t_stacks[0]
        own_sb = sb("own_sb", [GROUP, PAIR], F32)
        warm = sb("warm", [P, HALF], mybir.dt.bfloat16)
        zeros = sb("zeros", [P, GROUP], mybir.dt.bfloat16)
        silu_warm = sb("silu_warm", [1, 1], F32)
        idx_raw = sb("idx_raw", [1, 2, SEQS], I32)
        idx_wrap = sb("idx_wrap", [1, 2, SEQS], I32)
        idx_sum = sb("idx_sum", [1, 2, SEQS], I32)
        idx = sb("idx", [1, 2, SEQS], I32)
        psum = ctx.enter_context(nc.psum_tensor("psum", [P, 8, HALF], F32))

        silu = x_full[:, HC - 1, :]
        silu_short = x_full[0:SHORT, HC - 2, :]
        a_gu_raw = x_full[:, 0, :]
        t_full = [x_full[0:GROUP, g, :] for g in range(2)]
        a_down_raw = x_full[:, 1:3, :].rearrange("p a b -> p (a b)")[:, 0:SEQS * FC * RANK]
        short_hi, short_lo = [v[:, FC - HC:FC, :].rearrange("p k (g q c) -> p k g q c", g=2, q=PAIRS_OF_SEQS) for v in (act_hi, act_lo)]
        a_down_hl = a_late[:, :].rearrange("p (f c) -> p f c", f=FC)
        A1 = HC * SEQS * GROUP
        a_one_hi = a_late[:, 0:A1].rearrange("p (k c) -> p k c", k=HC)
        a_one_lo = a_late[:, A1:2 * A1].rearrange("p (k c) -> p k c", k=HC)
        b_one_stack = a_late[0:STACK, 2 * A1:2 * A1 + H]
        b_down_raw = b_raw[0:STACK, :, :].rearrange("p a (b c) -> p (a b) c", c=H)
        b_down_stack = b_stack[:, :, :].rearrange("p a (b c) -> p (a b) c", c=H)
        a_one_raw = b_raw[:, 0, 0:A1]
        b_one_raw = b_raw[0:STACK, 1, 0:H]

        x_loaded = [sem(f"x_loaded{i}") for i in range(X_PIECES)]
        w0_loaded = [sem(f"w0_loaded{k}") for k in range(HC)]
        w_loaded = [sem(f"w_loaded{s}") for s in range(2)]
        down_loaded = [sem(f"down_loaded{s}") for s in range(2)]
        one_loaded = [sem(f"one_loaded{k}") for k in range(HC)]
        idx_loaded = sem("idx_loaded")
        own_loaded = sem("own_loaded")
        warm_set = sem("warm_set")
        zeros_set = sem("zeros_set")
        short_loaded = sem("short_loaded")
        a_gu_loaded = sem("a_gu_loaded")
        a_down_loaded = sem("a_down_loaded")
        a_one_loaded = sem("a_one_loaded")
        b_loaded = sem("b_loaded")
        b_down_loaded = sem("b_down_loaded")
        b_one_loaded = sem("b_one_loaded")
        idx_step = sem("idx_step")
        x_hi_ready = sem("x_hi_ready")
        x_lo_ready = sem("x_lo_ready")
        x_full_ready = sem("x_full_ready")
        t_full_ready = sem("t_full_ready")
        w_hi_ready = sem("w_hi_ready")
        w_lo_ready = sem("w_lo_ready")
        down_hi_ready = sem("down_hi_ready")
        down_lo_ready = sem("down_lo_ready")
        one_hi_ready = sem("one_hi_ready")
        one_lo_ready = sem("one_lo_ready")
        silu_table = sem("silu_table")
        short_hi_ready = sem("short_hi_ready")
        short_lo_ready = sem("short_lo_ready")
        first_products_done = sem("first_products_done")
        a_down_hi_ready = sem("a_down_hi_ready")
        a_down_lo_ready = sem("a_down_lo_ready")
        a_one_hi_ready = sem("a_one_hi_ready")
        a_one_lo_ready = sem("a_one_lo_ready")
        b_hi_ready = sem("b_hi_ready")
        b_ready = sem("b_ready")
        b_down_hi_ready = sem("b_down_hi_ready")
        b_down_ready = sem("b_down_ready")
        b_one_hi_ready = sem("b_one_hi_ready")
        b_one_ready = sem("b_one_ready")
        t_done = sem("t_done")
        t_hi_ready = sem("t_hi_ready")
        t_again_ready = sem("t_again_ready")
        t_down_left = sem("t_down_left")
        t_one_hi_ready = sem("t_one_hi_ready")
        t_one_lo_ready = sem("t_one_lo_ready")
        t_lo_ready = sem("t_lo_ready")
        gate_done = sem("gate_done")
        gate_up_done = sem("gate_up_done")
        silu_done = sem("silu_done")
        mult_done = sem("mult_done")
        act_hi_ready = sem("act_hi_ready")
        act_lo_ready = sem("act_lo_ready")
        down_step_done = sem("down_step_done")
        down_done = sem("down_done")
        x1_ready = sem("x1_ready")
        x1_hi_ready = sem("x1_hi_ready")
        x1_lo_ready = sem("x1_lo_ready")
        out_done = sem("out_done")
        out_ready = sem("out_ready")
        stored = sem("stored")

        block = ctx.enter_context(nc.Block())

        x_pieces = [[slice(0, HALF), slice(HALF, TOK)]] + [[slice(0, TOK)]] * (HC - 1)

        out_pieces = [(o, slice(n * HALF, (n + 1) * HALF)) for o in range(HC) for n in range(HALVES)]
        out_pieces[-1:] = [(HC - 1, slice(TOK - HALF, TOK - PAIR)), (HC - 1, slice(TOK - PAIR, TOK))]

        def rows_of(f):
            return SHORT if f == 1 else P

        def gate_banks(s):
            return psum[:, 4 * s:4 * s + 2, :]

        def up_banks(s):
            return psum[:, 4 * s + 2:4 * s + 4, :]

        def first_banks(f):
            return psum[:, 2 * f:2 * f + 2, :], psum[:, 4 + 2 * f:6 + 2 * f, :]

        @block.sync
        def _(sp):
            def indices(t, n):
                _, values = nc.values_load_multi_w_load_instructions(
                    idx[0:1, t, :], engines=OrderedEngineSet([sp.engine]), min_val=0, max_val=n - 1,
                    skip_runtime_bounds_check_because="VectorE has brought them into the range")
                return values

            def load_gate_up(f, slot):
                sp.dma_start(w_raw[:, slot, :], w_gate_up[bass.ds(f, 1), :, :].rearrange("a p n -> (a p) n")).then_inc(w_loaded[slot], 16)

            def load_b(pair, seq, chunks=2):
                for b in range(SEQS):
                    sp.dma_start(b_raw[b % 2:STACK:2, 0:chunks, b // 2 * 2 * P:(b // 2 + 1) * 2 * P],
                                 b_gate_up[bass.ds(seq[b], 1), bass.ds(pair, 1), :, 0:chunks, :]
                                 .rearrange("i f p c n -> (i f p) c n")).then_inc(b_loaded, 16)

            def load_down(f, slot):
                sp.dma_start(w_raw[:, 1, slot * H:(slot + 1) * H],
                             w_down[bass.ds(f, 1), :, :].rearrange("a p n -> (a p) n")).then_inc(down_loaded[slot], 16)

            def load_one(k, slot, half):
                sp.dma_start(w_raw[:, slot, half * H:(half + 1) * H], w_one[k * P:(k + 1) * P, :]).then_inc(one_loaded[k], 16)

            piece = 2 * H // PIECES
            i = 0
            for k in range(HC):
                sp.dma_start(w_raw[:, 0, k * piece:(k + 1) * piece],
                             w_gate_up[0, :, k * piece:(k + 1) * piece]).then_inc(w0_loaded[k], 16)
                for tok in x_pieces[k]:
                    sp.dma_start(x_full[:, k, tok], x_t[k * P:(k + 1) * P, tok]).then_inc(x_loaded[i], 16)
                    if i == 0:
                        sp.dma_start(idx_raw[:, :, :].rearrange("p t b -> p (t b)"), sequence_indices).then_inc(idx_loaded, 16)
                    i += 1
            sp.dma_start(w_raw[:, 1, :], w_gate_up[1, :, :]).then_inc(short_loaded, 16)
            sp.wait_ge(idx_step, 3)
            seq = indices(0, ADAPTERS)
            sp.wait_ge(x_lo_ready, 2)
            for b in range(SEQS):
                sp.dma_start(a_gu_raw[:, b * P:(b + 1) * P],
                             a_gate_up[bass.ds(seq[b], 1), :, :].rearrange("i p n -> (i p) n")).then_inc(a_gu_loaded, 16)
            sp.dma_start(own_sb[:, :], own).then_inc(own_loaded, 16)
            load_b(0, seq)
            sp.wait_ge(w_lo_ready, PIECES)
            load_gate_up(2, 0)
            sp.wait_ge(short_lo_ready, 6)
            with sp.Fori(1, PAIRS) as pair:
                sp.wait_ge(b_ready, 2 * pair)
                load_b(pair, seq)
                for s in range(2):
                    sp.wait_ge(w_lo_ready, PIECES + 2 * pair + s - 2)
                    load_gate_up(2 * pair + 1 + s, 1 - s)
            sp.wait_ge(b_ready, FC - 1)
            load_b(PAIRS, seq, chunks=1)
            sp.wait_ge(t_again_ready, 2)
            sp.wait_ge(t_lo_ready, 2)
            sp.wait_ge(mult_done, 2)
            for b in range(SEQS):
                sp.dma_start(a_down_raw[:, b * FC * RANK:(b + 1) * FC * RANK],
                             a_down[bass.ds(seq[b], 1), :, :].rearrange("i p n -> (i p) n")).then_inc(a_down_loaded, 16)

            for f in range(2):
                if f == 0:
                    sp.wait_ge(w_lo_ready, PIECES + FC - 3)
                load_down(f, f)
            sp.wait_ge(w_lo_ready, PIECES + FC - 2)
            load_one(0, 0, 0)
            load_one(1, 0, 1)
            sp.wait_ge(b_ready, FC)
            for b in range(SEQS):
                sp.dma_start(b_down_raw[b % 2:STACK:2, b // 2, :],
                             b_down[bass.ds(seq[b], 1), :, :].rearrange("i p n -> (i p) n")).then_inc(b_down_loaded, 16)
            for f in (2, 3):
                sp.wait_ge(down_lo_ready, f - 1)
                load_down(f, f % 2)
            label = indices(1, LABELERS)
            sp.wait_ge(b_down_ready, 1)
            for b in range(SEQS):
                sp.dma_start(a_one_raw[:, b * P:(b + 1) * P],
                             a_one[bass.ds(label[b], 1), :, :].rearrange("i p n -> (i p) n")).then_inc(a_one_loaded, 16)
            sp.dma_start(b_one_raw, b_one).then_inc(b_one_loaded, 16)
            with sp.Fori(2, PAIRS) as pair:
                for s in range(2):
                    sp.wait_ge(down_lo_ready, 2 * pair + s - 1)
                    load_down(2 * pair + s, s)
            sp.wait_ge(down_lo_ready, FC - 2)
            load_down(FC - 1, 0)
            sp.wait_ge(down_lo_ready, FC - 1)
            load_one(2, 1, 1)
            sp.wait_ge(down_lo_ready, FC)
            load_one(3, 1, 0)

            for i, (o, tok) in enumerate(out_pieces):
                sp.wait_ge(out_ready, i + 1)
                sp.dma_start(out_t[o * P:(o + 1) * P, tok], x_full[:, o, tok]).then_inc(stored, 16)
            sp.wait_ge(stored, 16 * len(out_pieces))

        @block.gpsimd
        def _(pool):
            def b_lo(f, slot):
                pool.wait_ge(b_hi_ready, f + 1)
                last = b_stack[2 * GROUP:STACK, slot, :]
                nc.gpsimd.tensor_tensor(last, b_raw[2 * GROUP:STACK, slot, :], last.bitcast(F32), ALU.subtract).then_inc(b_ready, 1)

            nc.gpsimd.memset(warm[:, :], 1.0).then_inc(warm_set, 1)
            nc.gpsimd.memset(zeros[:, :], 0.0).then_inc(zeros_set, 1)

            pool.wait_ge(warm_set, 1)
            pool.wait_ge(zeros_set, 1)
            with pool.Fori(0, PAIRS) as pair:
                b_lo(2 * pair, 0)
                b_lo(2 * pair + 1, 1)
            b_lo(FC - 1, 0)

            pool.wait_ge(b_down_hi_ready, 1)
            last = b_down_stack[2 * GROUP:STACK, :, :]
            nc.gpsimd.tensor_tensor(last, b_down_raw[2 * GROUP:STACK, :, :], last.bitcast(F32), ALU.subtract).then_inc(b_down_ready, 1)
            pool.wait_ge(b_down_ready, 1)
            pool.wait_ge(t_again_ready, 3)
            pool.wait_ge(t_lo_ready, 3)
            pool.wait_ge(mult_done, FC)
            for k in range(HC):
                nc.gpsimd.tensor_tensor(x_full[:, k, :], x_hi[:, k, :].bitcast(F32), x_lo[:, k, :].bitcast(F32),
                                        ALU.add).then_inc(x_full_ready, 1)
            pool.wait_ge(x_full_ready, HC)
            pool.wait_ge(b_one_hi_ready, 1)
            last = b_one_stack[2 * GROUP:STACK, :]
            nc.gpsimd.tensor_tensor(last, b_one_raw[2 * GROUP:STACK, :], last.bitcast(F32), ALU.subtract).then_inc(b_one_ready, 1)

        def in_stack(part, j):
            rows = t_stack[GROUP * part:GROUP * (part + 1), :].rearrange("p (n c) -> p n c", n=HALVES)
            return rows[:, :, j * P:(j + 1) * P]

        def t_of_sequences(j):
            return t_banks[GROUP * j:GROUP * (j + 1), :, j * P:(j + 1) * P]

        def t_of_pairs(banks, q):
            return banks[GROUP * q:GROUP * (q + 1), :, q // 2 * PAIR:(q // 2 + 1) * PAIR]

        def short_parts(part, g):
            weights = w_raw[:, 1, :].rearrange("p (k g q c) -> p k g q c", k=HC, g=2, q=1)[:, :, g, :, 0:SHORT]
            yield part[:, :, g, :, 0:SHORT], weights.broadcast_to((P, HC, PAIRS_OF_SEQS, SHORT))
            a = a_gu_raw.rearrange("p (q s k g r) -> p k q s g r", s=2, k=HC, g=2, r=RANK)
            for s in range(2):
                yield part[:, :, g, :, SHORT:P].rearrange("p k q (r s) -> p k q r s", s=2)[:, :, :, :, s], a[:, :, :, s, g, :]

        def a_down_loaded_columns(s):
            return a_down_raw.rearrange("p (q s f r) -> p f q s r", s=2, f=FC, r=RANK)[:, :, :, s, :]

        def a_down_parts(ap_of_columns, part, s):
            return ap_of_columns.rearrange("p f (q h r s) -> p f q h r s", h=2, r=RANK, s=2)[:, :, :, part, :, s]

        t_banks = psum[:, bank_of(HC - 1):bank_of(HC - 1) + 2, :]

        @block.scalar
        def _(act):
            piece = 2 * H // PIECES

            def hi_of_weights(loads, f, slot):
                act.wait_ge(w_loaded[slot], loads)
                nc.scalar.copy(w_hi[:, slot, :], w_raw[:, slot, :]).then_inc(w_hi_ready, 1)

            def hi_of_b(pair, slot):
                act.wait_ge(b_loaded, 16 * SEQS * (pair + 1))
                nc.scalar.copy(b_stack[:, slot, :], b_raw[0:STACK, slot, :]).then_inc(b_hi_ready, 1)

            def hi_of_tile(hi, raw, ready):
                nc.scalar.copy(hi, raw).then_inc(ready, 1)

            def hi_of_t(use, g):
                act.wait_ge(t_full_ready, use + 1)
                nc.scalar.copy(t_stacks[g][0:GROUP, :], t_full[g]).then_inc(t_hi_ready, 1)
                nc.scalar.copy(t_stacks[g][2 * GROUP:STACK, :], t_full[g]).then_inc(t_again_ready, 1)

            def hi_of_last_t():
                act.wait_ge(t_done, 4)
                for j in range(PER_HALF):
                    nc.scalar.activation(in_stack(0, j), t_of_sequences(j), ACT.Copy,
                                         scale=LORA_SCALE).then_inc(t_one_hi_ready, 1)
                act.wait_ge(t_one_hi_ready, PER_HALF)
                nc.scalar.copy(t_stack[2 * GROUP:STACK, :], t_stack[0:GROUP, :].bitcast(F32)).then_inc(t_again_ready, 1)

            def activate(f, banks):
                act.wait_ge(gate_done, f + 1)
                nc.scalar.activation(silu, banks.rearrange("p n c -> p (n c)"), ACT.Silu).then_inc(silu_done, 1)

            def hi_of_act(f, banks, rows=P):
                act.wait_ge(mult_done, f + 1)
                nc.scalar.copy(act_hi[0:rows, bass.ds(f, 1), :].rearrange("p a n -> p (a n)"),
                               banks[0:rows].rearrange("p n c -> p (n c)")).then_inc(act_hi_ready, 1)

            act.wait_ge(warm_set, 1)
            nc.scalar.activation(silu_warm[:, :], warm[0:1, 0:1], ACT.Silu).then_inc(silu_table, 1)
            i = 0
            for k in range(HC):
                act.wait_ge(w0_loaded[k], 16)
                cols = slice(k * piece, (k + 1) * piece)
                nc.scalar.copy(w_hi[:, 0, cols], w_raw[:, 0, cols]).then_inc(w_hi_ready, 1)
                for tok in x_pieces[k]:
                    act.wait_ge(x_loaded[i], 16)
                    nc.scalar.copy(x_hi[:, k, tok], x_full[:, k, tok]).then_inc(x_hi_ready, 1)
                    i += 1
            for g in range(2):
                for i, (hi, raw) in enumerate(short_parts(short_hi, g)):
                    if g == 0 and i == 0:
                        act.wait_ge(short_loaded, 16)
                    if g == 0 and i == 1:
                        act.wait_ge(a_gu_loaded, 16 * SEQS)
                    nc.scalar.copy(hi, raw).then_inc(short_hi_ready, 1)
            hi_of_b(0, 0)
            hi_of_b(0, 1)
            act.wait_ge(first_products_done, 1)
            hi_of_weights(16, 2, 0)
            hi_of_t(0, 0)
            activate(0, first_banks(0)[0])
            act.wait_ge(gate_done, 2)
            nc.scalar.activation(silu_short, first_banks(1)[0][0:SHORT].rearrange("p n c -> p (n c)"), ACT.Silu).then_inc(silu_done, 1)
            hi_of_t(1, 1)
            hi_of_weights(16, 3, 1)
            act.wait_ge(gate_up_done, 1)
            hi_of_b(1, 0)
            hi_of_act(0, first_banks(0)[1])
            hi_of_act(1, first_banks(1)[1], SHORT)

            def evacuate(f, s, pair_of_next):
                act.wait_ge(mult_done, f)
                activate(f, gate_banks(s))
                hi_of_act(f, up_banks(s))
                hi_of_b(pair_of_next, 1 - s)

            def step(f, s, pair_of_next):
                act.wait_ge(gate_up_done, f)
                hi_of_weights(16 * pair_of_next, f + 1, 1 - s)
                evacuate(f, s, pair_of_next)

            evacuate(2, 0, 1)
            with act.Fori(1, PAIRS - 1) as pair:
                step(2 * pair + 1, 1, pair + 1)
                step(2 * pair + 2, 0, pair + 1)
            step(FC - 2, 1, PAIRS)

            act.wait_ge(a_down_loaded, 16 * SEQS)
            for s in range(2):
                nc.scalar.copy(a_down_parts(a_down_hl, 0, s), a_down_loaded_columns(s)).then_inc(a_down_hi_ready, 1)

            def hi_of_down(f, loads, slot):
                act.wait_ge(down_loaded[slot], loads)
                cols = slice(slot * H, (slot + 1) * H)
                nc.scalar.copy(w_hi[:, 1, cols], w_raw[:, 1, cols]).then_inc(down_hi_ready, 1)

            def hi_of_one(k, slot, half):
                act.wait_ge(one_loaded[k], 16)
                cols = slice(half * H, (half + 1) * H)
                nc.scalar.copy(w_hi[:, slot, cols], w_raw[:, slot, cols]).then_inc(one_hi_ready, 1)

            act.wait_ge(gate_up_done, FC - 1)
            hi_of_down(0, 16, 0)
            hi_of_down(1, 16, 1)
            act.wait_ge(mult_done, FC - 1)
            activate(FC - 1, gate_banks(0))
            hi_of_act(FC - 1, up_banks(0))
            act.wait_ge(gate_up_done, FC)
            act.wait_ge(b_down_loaded, 16 * SEQS)
            nc.scalar.copy(b_down_stack, b_down_raw).then_inc(b_down_hi_ready, 1)
            hi_of_one(0, 0, 0)
            hi_of_one(1, 0, 1)
            hi_of_t(2, 0)
            with act.Fori(1, PAIRS) as pair:
                for s in range(2):
                    act.wait_ge(down_step_done, 2 * pair + s - 1)
                    hi_of_down(2 * pair + s, 16 * (pair + 1), s)
            act.wait_ge(down_step_done, FC - 2)
            hi_of_down(FC - 1, 16 * (PAIRS + 1), 0)
            act.wait_ge(a_one_loaded, 16 * SEQS)
            nc.scalar.copy(a_one_hi.rearrange("p k (b c) -> p k b c", b=SEQS),
                           a_one_raw.rearrange("p (b k c) -> p k b c", b=SEQS, k=HC)).then_inc(a_one_hi_ready, 1)
            act.wait_ge(b_one_loaded, 16)
            nc.scalar.copy(b_one_stack, b_one_raw).then_inc(b_one_hi_ready, 1)
            act.wait_ge(down_step_done, FC - 1)
            hi_of_one(2, 1, 1)
            for c in range(HC):
                act.wait_ge(x1_ready, c + 1)
                nc.scalar.copy(x_hi[:, c, :], x_full[:, c, :]).then_inc(x1_hi_ready, 1)
            act.wait_ge(down_done, HC)
            hi_of_one(3, 1, 0)
            hi_of_last_t()

        @block.vector
        def _(dve):
            piece = 2 * H // PIECES

            def lo(out, raw, hi, ready):
                nc.vector.tensor_tensor(out, raw, hi.bitcast(F32), ALU.subtract).then_inc(ready, 1)

            def lo_of_weights(f, slot):
                dve.wait_ge(w_hi_ready, PIECES + f - 1)
                lo(w_lo[:, slot, :], w_raw[:, slot, :], w_hi[:, slot, :], w_lo_ready)

            def own_of(pairs):
                return own_sb[:, :].rearrange("p (n c) -> p n c", n=1).broadcast_to((GROUP, pairs, PAIR))

            def t_of_group(out, banks, q):
                half_pairs = out.rearrange("p (n c) -> p n c", n=HALVES)[:, :, q // 2 * PAIR:(q // 2 + 1) * PAIR]
                return nc.vector.scalar_tensor_tensor(half_pairs, t_of_pairs(banks, q), LORA_SCALE, own_of(HALVES),
                                                      ALU.mult, ALU.mult)

            def lo_of_t(use, g):
                dve.wait_ge(t_hi_ready, use + 1)
                lo(t_stacks[g][GROUP:2 * GROUP, :], t_full[g], t_stacks[g][0:GROUP, :], t_lo_ready)

            def lo_of_last_t():
                for j in range(PER_HALF):
                    dve.wait_ge(t_one_hi_ready, j + 1)
                    nc.vector.scalar_tensor_tensor(in_stack(1, j), t_of_sequences(j), LORA_SCALE,
                                                   in_stack(0, j).bitcast(F32), ALU.mult, ALU.subtract
                                                   ).then_inc(t_one_lo_ready, 1)

            def multiply(f, banks, silu=silu, rows=P):
                dve.wait_ge(silu_done, f + 1)
                dve.wait_ge(gate_up_done, f + 1)
                up = banks[0:rows].rearrange("p n c -> p (n c)")
                nc.vector.tensor_tensor(up, silu, up, ALU.mult).then_inc(mult_done, 1)

            def lo_of_act(f, banks, rows=P):
                dve.wait_ge(act_hi_ready, f + 1)
                at = bass.ds(f, 1)
                nc.vector.tensor_tensor(act_lo[0:rows, at, :].rearrange("p a n -> p (a n)"),
                                        banks[0:rows].rearrange("p n c -> p (n c)"),
                                        act_hi[0:rows, at, :].rearrange("p a n -> p (a n)").bitcast(F32),
                                        ALU.subtract).then_inc(act_lo_ready, 1)

            def wrap_indices():
                dve.wait_ge(idx_loaded, 16)
                for t, n in ((0, ADAPTERS), (1, LABELERS)):
                    last = nc.vector.tensor_scalar(idx_wrap[:, t, :], idx_raw[:, t, :], 0, n, ALU.is_lt, ALU.mult)
                last.then_inc(idx_step, 1)
                dve.wait_ge(idx_step, 1)
                nc.vector.tensor_tensor(idx_sum[:, :, :], idx_raw[:, :, :], idx_wrap[:, :, :], ALU.add).then_inc(idx_step, 1)
                dve.wait_ge(idx_step, 2)
                for t, n in ((0, ADAPTERS), (1, LABELERS)):
                    last = nc.vector.tensor_scalar(idx[:, t, :], idx_sum[:, t, :], 0, n - 1, ALU.max, ALU.min)
                last.then_inc(idx_step, 1)

            i = 0
            for k in range(HC):
                dve.wait_ge(w_hi_ready, k + 1)
                cols = slice(k * piece, (k + 1) * piece)
                lo(w_lo[:, 0, cols], w_raw[:, 0, cols], w_hi[:, 0, cols], w_lo_ready)
                for tok in x_pieces[k]:
                    dve.wait_ge(x_hi_ready, i + 1)
                    lo(x_lo[:, k, tok], x_full[:, k, tok], x_hi[:, k, tok], x_lo_ready)
                    i += 1
                if k == 0:
                    wrap_indices()
            for g in range(2):
                for i, ((out, raw), (hi, _)) in enumerate(zip(short_parts(short_lo, g), short_parts(short_hi, g))):
                    dve.wait_ge(short_hi_ready, 3 * g + i + 1)
                    lo(out, raw, hi, short_lo_ready)
            lo_of_weights(2, 0)

            def t_of_short(g):
                dve.wait_ge(t_done, g + 1)
                values = first_banks(1)[g][SHORT:P].rearrange("p n (j c) -> p (n j) c", c=PAIR)
                nc.vector.scalar_tensor_tensor(t_full[g].rearrange("p (q c) -> p q c", c=PAIR), values, LORA_SCALE,
                                               own_of(PAIRS_OF_SEQS), ALU.mult, ALU.mult).then_inc(t_full_ready, 1)
                lo_of_t(g, g)

            dve.wait_ge(own_loaded, 16)
            dve.wait_ge(short_lo_ready, 6)
            t_of_short(0)
            t_of_short(1)
            lo_of_weights(3, 1)
            multiply(0, first_banks(0)[1])
            multiply(1, first_banks(1)[1], silu_short, SHORT)
            lo_of_act(0, first_banks(0)[1])
            lo_of_act(1, first_banks(1)[1], SHORT)

            def evacuate(f, s):
                multiply(f, up_banks(s))
                lo_of_act(f, up_banks(s))

            def step(f, s):
                lo_of_weights(f + 1, 1 - s)
                evacuate(f, s)

            evacuate(2, 0)
            with dve.Fori(1, PAIRS - 1) as pair:
                step(2 * pair + 1, 1)
                step(2 * pair + 2, 0)
            step(FC - 2, 1)
            for s in range(2):
                dve.wait_ge(a_down_hi_ready, s + 1)
                lo(a_down_parts(a_down_hl, 1, s), a_down_loaded_columns(s), a_down_parts(a_down_hl, 0, s), a_down_lo_ready)

            def lo_of_down(f, slot):
                dve.wait_ge(down_hi_ready, f + 1)
                cols = slice(slot * H, (slot + 1) * H)
                lo(w_lo[:, 1, cols], w_raw[:, 1, cols], w_hi[:, 1, cols], down_lo_ready)

            def lo_of_one(k, slot, half):
                dve.wait_ge(one_hi_ready, k + 1)
                cols = slice(half * H, (half + 1) * H)
                lo(w_lo[:, slot, cols], w_raw[:, slot, cols], w_hi[:, slot, cols], one_lo_ready)

            lo_of_down(0, 0)
            lo_of_down(1, 1)
            evacuate(FC - 1, 0)
            lo_of_one(0, 0, 0)
            lo_of_one(1, 0, 1)
            dve.wait_ge(t_done, 3)
            for q in range(2 * HALVES):
                last = t_of_group(t_full[q % 2], t_banks, q)
            last.then_inc(t_down_left, 1)
            dve.wait_ge(t_down_left, 1)
            nc.vector.tensor_tensor(t_full[0], t_full[0], t_full[1], ALU.add).then_inc(t_full_ready, 1)
            lo_of_t(2, 0)
            with dve.Fori(1, PAIRS) as pair:
                lo_of_down(2 * pair, 0)
                lo_of_down(2 * pair + 1, 1)
            lo_of_down(FC - 1, 0)
            dve.wait_ge(a_one_hi_ready, 1)
            lo(a_one_lo.rearrange("p k (b c) -> p k b c", b=SEQS), a_one_raw.rearrange("p (b k c) -> p k b c", b=SEQS, k=HC),
               a_one_hi.rearrange("p k (b c) -> p k b c", b=SEQS), a_one_lo_ready)
            lo_of_one(2, 1, 1)
            def add_x(c):
                dve.wait_ge(down_done, c + 1)
                dve.wait_ge(x_full_ready, c + 1)
                at = psum[:, bank_of(c):bank_of(c) + 2, :].rearrange("p n c -> p (n c)")
                nc.vector.tensor_tensor(x_full[:, c, :], at, x_full[:, c, :], ALU.add).then_inc(x1_ready, 1)

            def lo_of_x1(c):
                dve.wait_ge(x1_hi_ready, c + 1)
                lo(x_lo[:, c, :], x_full[:, c, :], x_hi[:, c, :], x1_lo_ready)

            add_x(0)
            for c in range(1, HC):
                add_x(c)
                lo_of_x1(c - 1)
            lo_of_x1(HC - 1)
            lo_of_one(3, 1, 0)
            lo_of_last_t()
            for i, (o, tok) in enumerate(out_pieces):
                dve.wait_ge(out_done, HALVES * o + tok.start // HALF + 1)
                at = psum[:, bank_of(o) + tok.start // HALF, tok.start % HALF:(tok.stop - 1) % HALF + 1]
                nc.vector.tensor_tensor(x_full[:, o, tok], at, x_full[:, o, tok], ALU.add).then_inc(out_ready, 1)

        @block.tensor
        def _(pe):
            def product(out, w_parts, v_parts, first):
                (w_h, w_l), (v_h, v_l) = w_parts, v_parts
                for w, v in ((w_h, v_h), (w_h, v_l), (w_l, v_h)):
                    for n in range(HALVES):
                        mm = nc.tensor.matmul(out[:, n, :], w, v[:, n * HALF:(n + 1) * HALF],
                                              start=first and w is w_h and v is v_h, stop=False)
                return mm

            def t_product(out, a_h, a_l, v_h, v_l, k, first, last):
                for n in range(HALVES):
                    cols = slice(n * P, (n + 1) * P)
                    tok = slice(n * HALF, (n + 1) * HALF)
                    for w, v in ((a_h, v_h), (a_h, v_l), (a_l, v_h)):
                        mm = nc.tensor.matmul(out[:, n, :], w[:, k, cols], v[:, k, tok],
                                              start=first and w is a_h and v is v_h, stop=last and w is a_l)
                return mm

            def adapters(out, stack_of, t):
                for q in range(PAIRS_OF_SEQS):
                    n, j = divmod(q, 2)
                    mm = nc.tensor.matmul(out[:, n, j * PAIR:(j + 1) * PAIR], stack_of(q), t[:, q * PAIR:(q + 1) * PAIR],
                                          start=False, stop=j == 1)
                return mm

            def gate_up_chunk(k, s, g, out):
                cols = slice((2 * k + g) * P, (2 * k + g + 1) * P)
                return product(out, (w_hi[:, s, cols], w_lo[:, s, cols]), (x_hi[:, k, :], x_lo[:, k, :]), k == 0)

            def gate_up_adapters(f, s, g, out, short=False):
                pe.wait_ge(b_ready, f + 1)
                if short:
                    for n in range(HALVES):
                        nc.tensor.matmul(out[SHORT:P, n, :], zeros[:, :], warm[:, :], start=True, stop=False)
                adapters(out, lambda q: b_stack[:, s, (2 * q + g) * P:(2 * q + g + 1) * P], t_stacks[g]
                         ).then_inc((gate_done, gate_up_done)[g], 1)

            def short_chunk(k, g):
                for q in range(PAIRS_OF_SEQS):
                    n, j = divmod(q, 2)
                    tok = slice(q * PAIR, (q + 1) * PAIR)
                    out = first_banks(1)[g][:, n, j * PAIR:(j + 1) * PAIR]
                    for w, v in ((short_hi, x_hi), (short_hi, x_lo), (short_lo, x_hi)):
                        mm = nc.tensor.matmul(out, w[:, k, g, q, :], v[:, k, tok],
                                         start=k == 0 and j == 0 and w is short_hi and v is x_hi, stop=False)
                    if k == HC - 1 and j == 1:
                        mm = nc.tensor.matmul(out[SHORT:P, 0:GROUP], zeros[:, :], zeros[:, :], start=False, stop=True)
                return mm

            def step(f, s):
                pe.wait_ge(w_hi_ready, PIECES + f - 1)
                pe.wait_ge(w_lo_ready, PIECES + f - 1)
                pe.wait_ge(silu_done, f - 1)
                pe.wait_ge(act_lo_ready, f - 1)
                for k in range(HC):
                    for g, out in enumerate((gate_banks(s), up_banks(s))):
                        gate_up_chunk(k, s, g, out)
                for g, out in enumerate((gate_banks(s), up_banks(s))):
                    gate_up_adapters(f, s, g, out)

            pe.wait_ge(warm_set, 1)
            for i in range(WARM_UP):
                nc.tensor.matmul(psum[:, 7, :], warm[:, 0:P], warm[:, :], start=True, stop=True)

            pe.wait_ge(w_hi_ready, 1)
            for n, tok in enumerate(x_pieces[0]):
                pe.wait_ge(x_hi_ready, n + 1)
                for w, v in ((w_hi, x_hi), (w_lo, x_hi), (w_hi, x_lo)):
                    if n == 0 and w is w_lo:
                        pe.wait_ge(w_lo_ready, 1)
                    if v is x_lo:
                        pe.wait_ge(x_lo_ready, n + 1)
                    for g, out in enumerate(first_banks(0)):
                        nc.tensor.matmul(out[:, n, :], w[:, 0, g * P:(g + 1) * P], v[:, 0, tok],
                                         start=w is w_hi and v is x_hi, stop=False)
            for k in range(1, HC):
                pe.wait_ge(w_hi_ready, k + 1)
                pe.wait_ge(w_lo_ready, k + 1)
                pe.wait_ge(x_hi_ready, k + 2)
                pe.wait_ge(x_lo_ready, k + 2)
                for g, out in enumerate(first_banks(0)):
                    mm = gate_up_chunk(k, 0, g, out)
            mm.then_inc(first_products_done, 1)
            pe.wait_ge(zeros_set, 1)
            for g in range(2):
                for k in range(HC):
                    if k == 0:
                        pe.wait_ge(short_hi_ready, 3 * (g + 1))
                        pe.wait_ge(short_lo_ready, 3 * (g + 1))
                    if g == 1 and k == HC - 1:
                        pe.wait_ge(t_again_ready, 1)
                        pe.wait_ge(t_lo_ready, 1)
                        for f in range(2):
                            gate_up_adapters(f, f, 0, first_banks(f)[0], short=f == 1)
                    mm = short_chunk(k, g)
                mm.then_inc(t_done, 1)
            pe.wait_ge(w_hi_ready, PIECES + 1)
            pe.wait_ge(w_lo_ready, PIECES + 1)
            pe.wait_ge(silu_done, 1)
            for k in range(HC):
                gate_up_chunk(k, 0, 0, gate_banks(0))
            pe.wait_ge(t_again_ready, 2)
            pe.wait_ge(t_lo_ready, 2)
            for f in range(2):
                gate_up_adapters(f, f, 1, first_banks(f)[1], short=f == 1)
            pe.wait_ge(silu_done, 2)
            for k in range(HC):
                gate_up_chunk(k, 0, 1, up_banks(0))
            for g, out in enumerate((gate_banks(0), up_banks(0))):
                gate_up_adapters(2, 0, g, out)
            step(3, 1)
            with pe.Fori(2, PAIRS) as pair:
                step(2 * pair, 0)
                step(2 * pair + 1, 1)
            step(FC - 1, 0)

            pe.wait_ge(a_down_lo_ready, 2)
            pe.wait_ge(act_lo_ready, FC - 1)
            for f in range(FC):
                if f == FC - 1:
                    pe.wait_ge(act_lo_ready, FC)
                for n in range(HALVES):
                    for v in (act_hi, act_lo):
                        mm = nc.tensor.matmul(t_banks[:, n, :],
                                              a_down_hl[0:rows_of(f), f, n * P:(n + 1) * P],
                                              v[0:rows_of(f), f, n * HALF:(n + 1) * HALF],
                                              start=f == 0 and v is act_hi, stop=f == FC - 1 and v is act_lo)
            mm.then_inc(t_done, 1)

            def banks(c):
                return psum[:, bank_of(c):bank_of(c) + 2, :]

            def down_chunk(f, slot, c, first=False, rows=P):
                cols = slice(slot * H + c * P, slot * H + (c + 1) * P)
                v_parts = [v[0:rows, bass.ds(f, 1), :].rearrange("p a n -> p (a n)") for v in (act_hi, act_lo)]
                return product(banks(c), (w_hi[0:rows, 1, cols], w_lo[0:rows, 1, cols]), v_parts, first)

            def down_step(f, slot, first=False, rows=P):
                pe.wait_ge(down_hi_ready, f + 1)
                pe.wait_ge(down_lo_ready, f + 1)
                for c in range(HC):
                    if first and c == HC - 1:
                        pe.wait_ge(t_down_left, 1)
                    mm = down_chunk(f, slot, c, first, rows)
                mm.then_inc(down_step_done, 1)

            down_step(0, 0, first=True)
            down_step(1, 1, rows=SHORT)
            with pe.Fori(1, PAIRS) as pair:
                down_step(2 * pair, 0)
                down_step(2 * pair + 1, 1)
            pe.wait_ge(down_hi_ready, FC)
            pe.wait_ge(down_lo_ready, FC)
            pe.wait_ge(t_again_ready, 3)
            pe.wait_ge(t_lo_ready, 3)
            pe.wait_ge(b_down_ready, 1)
            for c in range(HC):
                down_chunk(FC - 1, 0, c)
                adapters(banks(c), lambda q: b_down_stack[:, q, c * P:(c + 1) * P], t_stack).then_inc(down_done, 1)

            place = [(0, 0), (0, 1), (1, 1), (1, 0)]

            def one_chunk(k, o):
                slot, half = place[k]
                cols = slice(half * H + o * P, half * H + (o + 1) * P)
                product(banks(o), (w_hi[:, slot, cols], w_lo[:, slot, cols]), (x_hi[:, k, :], x_lo[:, k, :]), k == 0)

            pe.wait_ge(a_one_hi_ready, 1)
            pe.wait_ge(a_one_lo_ready, 1)
            for k in range(HC):
                pe.wait_ge(one_hi_ready, k + 1)
                pe.wait_ge(one_lo_ready, k + 1)
                pe.wait_ge(x1_hi_ready, k + 1)
                pe.wait_ge(x1_lo_ready, k + 1)
                if k == HC - 1:
                    t_product(t_banks, a_one_hi, a_one_lo, x_hi, x_lo, k, False, True).then_inc(t_done, 1)
                for o in range(HC - 1):
                    if k == 0:
                        pe.wait_ge(x1_ready, o + 1)
                    one_chunk(k, o)
                if k == 0:
                    pe.wait_ge(x1_ready, HC)
                if k < HC - 1:
                    t_product(t_banks, a_one_hi, a_one_lo, x_hi, x_lo, k, k == 0, False)
            pe.wait_ge(b_one_ready, 1)
            pe.wait_ge(t_one_lo_ready, PER_HALF)
            pe.wait_ge(t_again_ready, 4)
            for o in range(HC):
                for n in range(HALVES):
                    tok = slice(n * HALF, (n + 1) * HALF)
                    if o == HC - 1:
                        for k in range(HC):
                            slot, half = place[k]
                            cols = slice(half * H + o * P, half * H + (o + 1) * P)
                            for w, v in ((w_hi, x_hi), (w_hi, x_lo), (w_lo, x_hi)):
                                nc.tensor.matmul(banks(o)[:, n, :], w[:, slot, cols], v[:, k, tok],
                                                 start=k == 0 and w is w_hi and v is x_hi, stop=False)
                    nc.tensor.matmul(banks(o)[:, n, :], b_one_stack[:, o * P:(o + 1) * P], t_stack[:, tok],
                                     start=False, stop=True).then_inc(out_done, 1)


def kernel(x, itok_B_2_6, itok_B_0_2, L0_cond_W_gate, L0_cond_W_up, L0_cond_W_down, L0_cond_A_gate, L0_cond_B_gate,
           L0_cond_A_up, L0_cond_B_up, L0_cond_A_down, L0_cond_B_down, L1_cond_W, L1_cond_lora_A, L1_cond_lora_B_w):
    import numpy as np
    import concourse.bacc as bacc
    from concourse.bass_utils import run_bass_kernel_spmd

    def in_chunks(a, axis):
        a = np.moveaxis(np.asarray(a), axis, 0)
        a = np.concatenate([a[:P + SHORT], np.zeros((P - SHORT,) + a.shape[1:], a.dtype), a[P + SHORT:]])
        return np.moveaxis(a, 0, axis)

    gate_up = np.stack([in_chunks(w, 0).reshape(FC, P, HC, P) for w in (L0_cond_W_gate, L0_cond_W_up)])
    gate_up = gate_up.transpose(1, 4, 3, 0, 2).reshape(FC, P, 2 * H)
    down = in_chunks(L0_cond_W_down, 1).T.reshape(FC, P, H)
    one = np.asarray(L1_cond_W).T
    a_gate_up = np.concatenate([np.asarray(L0_cond_A_gate)[0], np.asarray(L0_cond_A_up)[0]], 1)
    a_gate_up = a_gate_up.reshape(ADAPTERS, GROUP, HC, P).transpose(0, 3, 2, 1).reshape(ADAPTERS, P, HC * GROUP)
    a_down = in_chunks(np.asarray(L0_cond_A_down)[0], 2).reshape(ADAPTERS, RANK, FC, P).transpose(0, 3, 2, 1)
    a_down = a_down.reshape(ADAPTERS, P, FC * RANK)
    a_one = np.asarray(L1_cond_lora_A).reshape(LABELERS, HC, P, GROUP).transpose(0, 2, 1, 3).reshape(LABELERS, P, HC * GROUP)
    b_gate_up = np.stack([in_chunks(np.asarray(b)[0], 1).reshape(ADAPTERS, FC, P, RANK) for b in (L0_cond_B_gate, L0_cond_B_up)])
    b_gate_up = np.tile(b_gate_up.transpose(1, 2, 4, 0, 3).reshape(ADAPTERS, FC, RANK, 2 * P), (1, 1, 3, 1))
    b_gate_up = np.pad(b_gate_up, [(0, 0), (0, FC % 2), (0, 0), (0, 0)]).reshape(ADAPTERS, -1, 2, 3 * RANK, 2 * P)
    b_gate_up = b_gate_up.transpose(0, 1, 3, 2, 4)
    b_down = np.tile(np.asarray(L0_cond_B_down)[0].transpose(0, 2, 1), (1, 3, 1))
    b_one = np.tile(np.asarray(L1_cond_lora_B_w).T, (3, 1))
    own = np.tile(np.repeat(np.eye(2, dtype=np.float32), P, axis=1), (RANK, 1))

    nc = bacc.Bacc("TRN2", target_bir_lowering=False, num_devices=1)
    host = {
        "x_t": np.asarray(x).reshape(TOK, H).T,
        "sequence_indices": np.concatenate([np.asarray(itok_B_2_6), np.asarray(itok_B_0_2)]).reshape(1, 2 * SEQS),
        "own": own, "w_gate_up": gate_up, "w_down": down, "w_one": one,
        "a_gate_up": a_gate_up, "a_down": a_down, "a_one": a_one,
        "b_gate_up": b_gate_up, "b_down": b_down, "b_one": b_one,
    }
    host = {name: np.ascontiguousarray(a) for name, a in host.items()}
    aps = [nc.dram_tensor(name, a.shape, mybir.dt.from_np(a.dtype), kind="ExternalInput").ap() for name, a in host.items()]
    out_t = nc.dram_tensor("out_t", (H, TOK), F32, kind="ExternalOutput").ap()
    gated_lora_mlp_then_lora_linear(nc, *aps, out_t)
    result = run_bass_kernel_spmd(nc, [host], core_ids=[0])
    return result.results[0]["out_t"].T.reshape(SEQS, P, H)
```

```python
from contextlib import ExitStack

import concourse.bass as bass
from concourse import mybir
from concourse.bass import OrderedEngineSet

F32 = mybir.dt.float32
F32R = mybir.dt.float32r
I32 = mybir.dt.int32
ALU = mybir.AluOpType
ACT = mybir.ActivationFunctionType

P = 128
SEQS = 8
TOK = SEQS * P
HALF = 512
HALVES = TOK // HALF
H = 512
HC = H // P
F = 1376
FC = -(-F // P)
SHORT = F - (FC - 1) * P
RANK = 16
GROUP = 32
PAIR = 2 * P
PAIRS_OF_SEQS = SEQS // 2
STACK = 3 * GROUP
ADAPTERS = 16
LABELERS = 5
LORA_SCALE = 0.5
X_PIECES = HC + 2
PIECES = HC
PAIRS = (FC - 1) // 2
WARM_UP = 8


def bank_of(c):
    return (6 + 2 * c) % 8


def gated_lora_mlp_then_lora_linear(nc, x_t, sequence_indices, own, w_gate_up, w_down, w_one, a_gate_up, a_down, a_one,
                                    b_gate_up, b_down, b_one, out_t):
    with ExitStack() as ctx:
        def sb(name, shape, dt):
            return ctx.enter_context(nc.sbuf_tensor(name, shape, dt))

        def sem(name):
            return ctx.enter_context(nc.semaphore(name))

        x_hi = sb("x_hi", [P, HC, TOK], F32R)
        x_lo = sb("x_lo", [P, HC, TOK], F32R)
        x_full = sb("x_full", [P, HC, TOK], F32)
        act_hi = sb("act_hi", [P, FC, TOK], F32R)
        act_lo = sb("act_lo", [P, FC, TOK], F32R)
        w_raw = sb("w_raw", [P, 2, 2 * H], F32)
        w_hi = sb("w_hi", [P, 2, 2 * H], F32R)
        w_lo = sb("w_lo", [P, 2, 2 * H], F32R)
        b_raw = sb("b_raw", [P, 2, PAIRS_OF_SEQS * 2 * P], F32)
        b_stacks = sb("b_stacks", [P, 2, PAIRS_OF_SEQS * 2 * P], F32R)
        b_stack = b_stacks[0:STACK, :, :]
        a_late = sb("a_late", [P, FC * SEQS * GROUP], F32R)
        t_both = sb("t_both", [P, 2, TOK], F32R)
        t_stacks = [t_both[0:STACK, g, :] for g in range(2)]
        t_stack = t_stacks[0]
        own_sb = sb("own_sb", [GROUP, PAIR], F32)
        warm = sb("warm", [P, HALF], mybir.dt.bfloat16)
        zeros = sb("zeros", [P, GROUP], mybir.dt.bfloat16)
        silu_warm = sb("silu_warm", [1, 1], F32)
        idx_raw = sb("idx_raw", [1, 2, SEQS], I32)
        idx_wrap = sb("idx_wrap", [1, 2, SEQS], I32)
        idx_sum = sb("idx_sum", [1, 2, SEQS], I32)
        idx = sb("idx", [1, 2, SEQS], I32)
        psum = ctx.enter_context(nc.psum_tensor("psum", [P, 8, HALF], F32))

        silu = x_full[:, HC - 1, :]
        silu_short = x_full[0:SHORT, HC - 2, :]
        a_gu_raw = x_full[:, 0, :]
        t_full = [x_full[0:GROUP, g, :] for g in range(2)]
        a_down_raw = x_full[:, 1:3, :].rearrange("p a b -> p (a b)")[:, 0:SEQS * FC * RANK]
        short_hi, short_lo = [v[:, FC - HC:FC, :].rearrange("p k (g q c) -> p k g q c", g=2, q=PAIRS_OF_SEQS) for v in (act_hi, act_lo)]
        a_down_hl = a_late[:, :].rearrange("p (f c) -> p f c", f=FC)
        A1 = HC * SEQS * GROUP
        a_one_hl = a_late[:, 0:2 * A1].rearrange("p (k q h s r) -> p k q h s r", k=HC, q=PAIRS_OF_SEQS, h=2, s=2)
        b_one_stack = a_late[0:STACK, 2 * A1:2 * A1 + H]
        b_down_raw = b_raw[SHORT:P, :, :].rearrange("p a (b c) -> p (a b) c", c=H)
        down_short_hi = b_stacks[:, :, :].rearrange("p a (b c) -> p (a b) c", c=H)
        down_short_lo = t_both[:, :, :].rearrange("p a (b c) -> p (a b) c", c=H)
        t_down = [x_full[SHORT:P, g, :] for g in range(2)]
        a_one_raw = b_raw[:, 0, 0:A1]
        b_one_raw = b_raw[0:STACK, 1, 0:H]
        t_one = b_raw[0:GROUP, 0, :]

        x_loaded = [sem(f"x_loaded{i}") for i in range(X_PIECES)]
        w0_loaded = [sem(f"w0_loaded{k}") for k in range(HC)]
        w_loaded = [sem(f"w_loaded{s}") for s in range(2)]
        down_loaded = [sem(f"down_loaded{s}") for s in range(2)]
        one_loaded = [sem(f"one_loaded{k}") for k in range(HC)]
        idx_loaded = sem("idx_loaded")
        own_loaded = sem("own_loaded")
        warm_set = sem("warm_set")
        zeros_set = sem("zeros_set")
        short_loaded = sem("short_loaded")
        a_gu_loaded = sem("a_gu_loaded")
        a_down_loaded = sem("a_down_loaded")
        a_one_loaded = sem("a_one_loaded")
        b_loaded = sem("b_loaded")
        b_down_loaded = sem("b_down_loaded")
        b_one_loaded = sem("b_one_loaded")
        idx_step = sem("idx_step")
        x_hi_ready = sem("x_hi_ready")
        x_lo_ready = sem("x_lo_ready")
        x_full_ready = sem("x_full_ready")
        t_full_ready = sem("t_full_ready")
        w_hi_ready = sem("w_hi_ready")
        w_lo_ready = sem("w_lo_ready")
        down_hi_ready = sem("down_hi_ready")
        down_lo_ready = sem("down_lo_ready")
        one_hi_ready = sem("one_hi_ready")
        one_lo_ready = sem("one_lo_ready")
        short_hi_ready = sem("short_hi_ready")
        short_lo_ready = sem("short_lo_ready")
        first_products_done = sem("first_products_done")
        a_down_hi_ready = sem("a_down_hi_ready")
        a_down_lo_ready = sem("a_down_lo_ready")
        a_one_hi_ready = sem("a_one_hi_ready")
        a_one_lo_ready = sem("a_one_lo_ready")
        b_hi_ready = sem("b_hi_ready")
        b_ready = sem("b_ready")
        b_down_hi_ready = sem("b_down_hi_ready")
        b_down_ready = sem("b_down_ready")
        b_one_hi_ready = sem("b_one_hi_ready")
        b_one_ready = sem("b_one_ready")
        t_done = sem("t_done")
        t_hi_ready = sem("t_hi_ready")
        t_again_ready = sem("t_again_ready")
        t_down_left = sem("t_down_left")
        t_down_ready = sem("t_down_ready")
        t_down_hi_ready = sem("t_down_hi_ready")
        t_down_lo_ready = sem("t_down_lo_ready")
        t_one_part_ready = sem("t_one_part_ready")
        t_lo_ready = sem("t_lo_ready")
        gate_done = sem("gate_done")
        gate_up_done = sem("gate_up_done")
        silu_done = sem("silu_done")
        mult_done = sem("mult_done")
        act_hi_ready = sem("act_hi_ready")
        act_lo_ready = sem("act_lo_ready")
        down_step_done = sem("down_step_done")
        down_done = sem("down_done")
        x1_ready = sem("x1_ready")
        x1_hi_ready = sem("x1_hi_ready")
        x1_lo_ready = sem("x1_lo_ready")
        out_done = sem("out_done")
        out_ready = sem("out_ready")
        stored = sem("stored")

        block = ctx.enter_context(nc.Block())

        x_pieces = [[slice(0, HALF), slice(HALF, TOK)]] * 2 + [[slice(0, TOK)]] * (HC - 2)

        out_pieces = [(o, slice(n * HALF, (n + 1) * HALF)) for o in range(HC) for n in range(HALVES)]
        out_pieces[-1:] = [(HC - 1, slice(TOK - HALF, TOK - PAIR)), (HC - 1, slice(TOK - PAIR, TOK))]

        def rows_of(f):
            return SHORT if f == 1 else P

        def gate_banks(s):
            return psum[:, 4 * s:4 * s + 2, :]

        def up_banks(s):
            return psum[:, 4 * s + 2:4 * s + 4, :]

        def first_banks(f):
            return psum[:, 2 * f:2 * f + 2, :], psum[:, 4 + 2 * f:6 + 2 * f, :]

        @block.sync
        def _(sp):
            def indices(t, n):
                _, values = nc.values_load_multi_w_load_instructions(
                    idx[0:1, t, :], engines=OrderedEngineSet([sp.engine]), min_val=0, max_val=n - 1,
                    skip_runtime_bounds_check_because="VectorE has brought them into the range")
                return values

            def load_gate_up(f, slot):
                sp.dma_start(w_raw[:, slot, :], w_gate_up[bass.ds(f, 1), :, :].rearrange("a p n -> (a p) n")).then_inc(w_loaded[slot], 16)

            def load_b(pair, seq, chunks=2):
                for b in range(SEQS):
                    sp.dma_start(b_raw[b % 2:STACK:2, 0:chunks, b // 2 * 2 * P:(b // 2 + 1) * 2 * P],
                                 b_gate_up[bass.ds(seq[b], 1), bass.ds(pair, 1), :, 0:chunks, :]
                                 .rearrange("i f p c n -> (i f p) c n")).then_inc(b_loaded, 16)

            def load_down(f, slot):
                sp.dma_start(w_raw[:, 1, slot * H:(slot + 1) * H],
                             w_down[bass.ds(f, 1), :, :].rearrange("a p n -> (a p) n")).then_inc(down_loaded[slot], 16)

            def load_one(k, slot, half):
                sp.dma_start(w_raw[:, slot, half * H:(half + 1) * H], w_one[k * P:(k + 1) * P, :]).then_inc(one_loaded[k], 16)

            piece = 2 * H // PIECES
            i = 0
            for k in range(HC):
                sp.dma_start(w_raw[:, 0, k * piece:(k + 1) * piece],
                             w_gate_up[0, :, k * piece:(k + 1) * piece]).then_inc(w0_loaded[k], 16)
                for tok in x_pieces[k]:
                    sp.dma_start(x_full[:, k, tok], x_t[k * P:(k + 1) * P, tok]).then_inc(x_loaded[i], 16)
                    if i == 0:
                        sp.dma_start(idx_raw[:, :, :].rearrange("p t b -> p (t b)"), sequence_indices).then_inc(idx_loaded, 16)
                    i += 1
            sp.dma_start(w_raw[:, 1, :], w_gate_up[1, :, :]).then_inc(short_loaded, 16)
            sp.wait_ge(idx_step, 3)
            seq = indices(0, ADAPTERS)
            sp.wait_ge(x_lo_ready, 2)
            for b in range(SEQS):
                sp.dma_start(a_gu_raw[:, b * P:(b + 1) * P],
                             a_gate_up[bass.ds(seq[b], 1), :, :].rearrange("i p n -> (i p) n")).then_inc(a_gu_loaded, 16)
            sp.dma_start(own_sb[:, :], own).then_inc(own_loaded, 16)
            sp.wait_ge(w_lo_ready, PIECES)
            load_gate_up(2, 0)
            load_b(0, seq)
            sp.wait_ge(short_lo_ready, 6)
            load_gate_up(3, 1)

            def load_next(pair, slots):
                sp.wait_ge(b_ready, 2 * pair)
                load_b(pair, seq)
                for s in slots:
                    sp.wait_ge(w_lo_ready, PIECES + 2 * pair + s - 1)
                    load_gate_up(2 * pair + 2 + s, s)

            with sp.Fori(1, PAIRS - 1) as pair:
                load_next(pair, (0, 1))
            load_next(PAIRS - 1, (0,))
            sp.wait_ge(b_ready, FC - 1)
            load_b(PAIRS, seq, chunks=1)
            sp.wait_ge(t_again_ready, 2)
            sp.wait_ge(t_lo_ready, 2)
            sp.wait_ge(mult_done, 2)
            for b in range(SEQS):
                sp.dma_start(a_down_raw[:, b * FC * RANK:(b + 1) * FC * RANK],
                             a_down[bass.ds(seq[b], 1), :, :].rearrange("i p n -> (i p) n")).then_inc(a_down_loaded, 16)

            sp.wait_ge(w_lo_ready, PIECES + FC - 3)
            load_down(0, 0)
            load_down(2, 1)
            sp.wait_ge(w_lo_ready, PIECES + FC - 2)
            load_one(0, 0, 0)
            load_one(1, 0, 1)
            sp.wait_ge(b_ready, FC)
            for b in range(SEQS):
                sp.dma_start(b_down_raw[b % 2:GROUP:2, b // 2, :],
                             b_down[bass.ds(seq[b], 1), :, :].rearrange("i p n -> (i p) n")).then_inc(b_down_loaded, 16)
            for i in (2, 3):
                sp.wait_ge(down_lo_ready, i - 1)
                load_down(i + 1, i % 2)
            label = indices(1, LABELERS)
            sp.wait_ge(b_down_ready, 1)
            for b in range(SEQS):
                sp.dma_start(a_one_raw[:, b * P:(b + 1) * P],
                             a_one[bass.ds(label[b], 1), :, :].rearrange("i p n -> (i p) n")).then_inc(a_one_loaded, 16)
            sp.dma_start(b_one_raw, b_one).then_inc(b_one_loaded, 16)
            with sp.Fori(2, PAIRS) as pair:
                for s in range(2):
                    sp.wait_ge(down_lo_ready, 2 * pair + s - 1)
                    load_down(2 * pair + s + 1, s)
            sp.wait_ge(down_lo_ready, FC - 2)
            load_down(1, 0)
            sp.wait_ge(down_lo_ready, FC - 1)
            load_one(2, 1, 1)
            sp.wait_ge(down_lo_ready, FC)
            load_one(3, 1, 0)

            for i, (o, tok) in enumerate(out_pieces):
                sp.wait_ge(out_ready, i + 1)
                sp.dma_start(out_t[o * P:(o + 1) * P, tok], x_full[:, o, tok]).then_inc(stored, 16)
            sp.wait_ge(stored, 16 * len(out_pieces))

        @block.gpsimd
        def _(pool):
            def b_lo(f, slot):
                pool.wait_ge(b_hi_ready, f + 1)
                last = b_stack[2 * GROUP:STACK, slot, :]
                nc.gpsimd.tensor_tensor(last, b_raw[2 * GROUP:STACK, slot, :], last.bitcast(F32), ALU.subtract).then_inc(b_ready, 1)

            nc.gpsimd.memset(warm[:, :], 1.0).then_inc(warm_set, 1)
            nc.gpsimd.memset(zeros[:, :], 0.0).then_inc(zeros_set, 1)

            pool.wait_ge(warm_set, 1)
            pool.wait_ge(zeros_set, 1)
            with pool.Fori(0, PAIRS) as pair:
                b_lo(2 * pair, 0)
                b_lo(2 * pair + 1, 1)
            b_lo(FC - 1, 0)

            pool.wait_ge(b_ready, FC)
            pool.wait_ge(t_down_hi_ready, 1)
            pool.wait_ge(t_down_lo_ready, 1)
            pool.wait_ge(mult_done, FC)
            for k in range(HC):
                nc.gpsimd.tensor_tensor(x_full[:, k, :], x_hi[:, k, :].bitcast(F32), x_lo[:, k, :].bitcast(F32),
                                        ALU.add).then_inc(x_full_ready, 1)
            pool.wait_ge(x_full_ready, HC)
            pool.wait_ge(b_one_hi_ready, 1)
            last = b_one_stack[2 * GROUP:STACK, :]
            nc.gpsimd.tensor_tensor(last, b_one_raw[2 * GROUP:STACK, :], last.bitcast(F32), ALU.subtract).then_inc(b_one_ready, 1)

        def t_one_of(q, tokens):
            return tokens_of(t_banks[GROUP * q:GROUP * (q + 1)].rearrange("p n c -> p (n c)"), tokens)

        def tokens_of(rows, s):
            return rows.rearrange("p (q s c) -> p q s c", s=2, c=P)[:, :, s, :]

        def t_of_pairs(banks, q):
            return banks[GROUP * q:GROUP * (q + 1), :, q // 2 * PAIR:(q // 2 + 1) * PAIR]

        def short_parts(part, g):
            weights = w_raw[:, 1, :].rearrange("p (k g q c) -> p k g q c", k=HC, g=2, q=1)[:, :, g, :, 0:SHORT]
            yield part[:, :, g, :, 0:SHORT], weights.broadcast_to((P, HC, PAIRS_OF_SEQS, SHORT))
            a = a_gu_raw.rearrange("p (q s k g r) -> p k q s g r", s=2, k=HC, g=2, r=RANK)
            for s in range(2):
                yield part[:, :, g, :, SHORT:P].rearrange("p k q (r s) -> p k q r s", s=2)[:, :, :, :, s], a[:, :, :, s, g, :]

        def down_short_loaded():
            tile = w_raw[0:SHORT, 1, 0:H].rearrange("p (q c) -> p q c", q=1)
            return tile.broadcast_to((SHORT, PAIRS_OF_SEQS, H))

        def a_one_loaded_columns(s):
            return a_one_raw.rearrange("p (q s k r) -> p k q s r", s=2, k=HC, r=GROUP)[:, :, :, s, :]

        def a_down_loaded_columns(s):
            return a_down_raw.rearrange("p (q s f r) -> p f q s r", s=2, f=FC, r=RANK)[:, :, :, s, :]

        def a_down_parts(ap_of_columns, part, s):
            return ap_of_columns.rearrange("p f (q h r s) -> p f q h r s", h=2, r=RANK, s=2)[:, :, :, part, :, s]

        t_banks = psum[:, bank_of(HC - 1):bank_of(HC - 1) + 2, :]

        @block.scalar
        def _(act):
            piece = 2 * H // PIECES

            def hi_of_weights(loads, slot):
                act.wait_ge(w_loaded[slot], loads)
                nc.scalar.copy(w_hi[:, slot, :], w_raw[:, slot, :]).then_inc(w_hi_ready, 1)

            def hi_of_b(pair, slot):
                act.wait_ge(b_loaded, 16 * SEQS * (pair + 1))
                nc.scalar.copy(b_stack[:, slot, :], b_raw[0:STACK, slot, :]).then_inc(b_hi_ready, 1)

            def hi_of_t(use, stack, t):
                act.wait_ge(t_full_ready, use + 1)
                nc.scalar.copy(stack[0:GROUP, :], t).then_inc(t_hi_ready, 1)
                nc.scalar.copy(stack[2 * GROUP:STACK, :], t).then_inc(t_again_ready, 1)

            def activate(f, banks):
                act.wait_ge(gate_done, f + 1)
                nc.scalar.activation(silu, banks.rearrange("p n c -> p (n c)"), ACT.Silu).then_inc(silu_done, 1)

            def hi_of_act(f, banks, rows=P):
                act.wait_ge(mult_done, f + 1)
                nc.scalar.copy(act_hi[0:rows, bass.ds(f, 1), :].rearrange("p a n -> p (a n)"),
                               banks[0:rows].rearrange("p n c -> p (n c)")).then_inc(act_hi_ready, 1)

            act.wait_ge(warm_set, 1)
            nc.scalar.activation(silu_warm[:, :], warm[0:1, 0:1], ACT.Silu)
            i = 0
            for k in range(HC):
                act.wait_ge(w0_loaded[k], 16)
                cols = slice(k * piece, (k + 1) * piece)
                nc.scalar.copy(w_hi[:, 0, cols], w_raw[:, 0, cols]).then_inc(w_hi_ready, 1)
                for tok in x_pieces[k]:
                    act.wait_ge(x_loaded[i], 16)
                    nc.scalar.copy(x_hi[:, k, tok], x_full[:, k, tok]).then_inc(x_hi_ready, 1)
                    i += 1
            for g in range(2):
                for i, (hi, raw) in enumerate(short_parts(short_hi, g)):
                    if g == 0 and i == 0:
                        act.wait_ge(short_loaded, 16)
                    if g == 0 and i == 1:
                        act.wait_ge(a_gu_loaded, 16 * SEQS)
                    nc.scalar.copy(hi, raw).then_inc(short_hi_ready, 1)
            act.wait_ge(first_products_done, 1)
            hi_of_weights(16, 0)
            hi_of_b(0, 0)
            hi_of_b(0, 1)
            hi_of_t(0, t_stacks[0], t_full[0])
            activate(0, first_banks(0)[0])
            act.wait_ge(gate_done, 2)
            nc.scalar.activation(silu_short, first_banks(1)[0][0:SHORT].rearrange("p n c -> p (n c)"), ACT.Silu).then_inc(silu_done, 1)
            hi_of_t(1, t_stacks[1], t_full[1])
            hi_of_weights(16, 1)
            act.wait_ge(gate_up_done, 1)
            hi_of_b(1, 0)
            hi_of_act(0, first_banks(0)[1])
            hi_of_act(1, first_banks(1)[1], SHORT)

            def evacuate(f, s, pair_of_next):
                act.wait_ge(mult_done, f)
                activate(f, gate_banks(s))
                hi_of_act(f, up_banks(s))
                hi_of_b(pair_of_next, 1 - s)

            def step(f, s, pair_of_next):
                act.wait_ge(gate_up_done, f)
                hi_of_weights(16 * pair_of_next, 1 - s)
                evacuate(f, s, pair_of_next)

            evacuate(2, 0, 1)
            with act.Fori(1, PAIRS - 1) as pair:
                step(2 * pair + 1, 1, pair + 1)
                step(2 * pair + 2, 0, pair + 1)
            step(FC - 2, 1, PAIRS)

            act.wait_ge(a_down_loaded, 16 * SEQS)
            for s in range(2):
                nc.scalar.copy(a_down_parts(a_down_hl, 0, s), a_down_loaded_columns(s)).then_inc(a_down_hi_ready, 1)

            def hi_of_down(loads, slot):
                act.wait_ge(down_loaded[slot], loads)
                cols = slice(slot * H, (slot + 1) * H)
                nc.scalar.copy(w_hi[:, 1, cols], w_raw[:, 1, cols]).then_inc(down_hi_ready, 1)

            def hi_of_one(k, slot, half):
                act.wait_ge(one_loaded[k], 16)
                cols = slice(half * H, (half + 1) * H)
                nc.scalar.copy(w_hi[:, slot, cols], w_raw[:, slot, cols]).then_inc(one_hi_ready, 1)

            act.wait_ge(gate_up_done, FC - 1)
            hi_of_down(16, 0)
            hi_of_down(16, 1)
            act.wait_ge(mult_done, FC - 1)
            activate(FC - 1, gate_banks(0))
            hi_of_act(FC - 1, up_banks(0))
            act.wait_ge(gate_up_done, FC)
            act.wait_ge(b_down_loaded, 16 * SEQS)
            nc.scalar.copy(down_short_hi[SHORT:P], b_down_raw).then_inc(b_down_hi_ready, 1)
            hi_of_one(0, 0, 0)
            hi_of_one(1, 0, 1)
            act.wait_ge(t_down_ready, 1)
            nc.scalar.copy(act_hi[SHORT:P, 1, :], t_down[0]).then_inc(t_down_hi_ready, 1)
            with act.Fori(1, PAIRS) as pair:
                for s in range(2):
                    act.wait_ge(down_step_done, 2 * pair + s - 1)
                    hi_of_down(16 * (pair + 1), s)
            act.wait_ge(down_loaded[0], 16 * (PAIRS + 1))
            nc.scalar.copy(down_short_hi[0:SHORT], down_short_loaded()).then_inc(down_hi_ready, 1)
            act.wait_ge(a_one_loaded, 16 * SEQS)
            for s in range(2):
                nc.scalar.copy(a_one_hl[:, :, :, 0, s, :], a_one_loaded_columns(s)).then_inc(a_one_hi_ready, 1)
            act.wait_ge(b_one_loaded, 16)
            nc.scalar.copy(b_one_stack, b_one_raw).then_inc(b_one_hi_ready, 1)
            act.wait_ge(down_step_done, FC - 1)
            hi_of_one(2, 1, 1)
            for c in range(HC):
                act.wait_ge(x1_ready, c + 1)
                nc.scalar.copy(x_hi[:, c, :], x_full[:, c, :]).then_inc(x1_hi_ready, 1)
            hi_of_one(3, 1, 0)
            act.wait_ge(t_done, 4)
            for s in range(2):
                nc.scalar.activation(tokens_of(t_one, s), t_one_of(s, s), ACT.Copy, scale=LORA_SCALE).then_inc(t_one_part_ready, 1)
            hi_of_t(2, t_stack, t_one)

        @block.vector
        def _(dve):
            piece = 2 * H // PIECES

            def lo(out, raw, hi, ready):
                nc.vector.tensor_tensor(out, raw, hi.bitcast(F32), ALU.subtract).then_inc(ready, 1)

            def lo_of_weights(f, slot):
                dve.wait_ge(w_hi_ready, PIECES + f - 1)
                lo(w_lo[:, slot, :], w_raw[:, slot, :], w_hi[:, slot, :], w_lo_ready)

            def own_of(pairs):
                return own_sb[:, :].rearrange("p (n c) -> p n c", n=1).broadcast_to((GROUP, pairs, PAIR))

            def t_of_group(out, banks, q):
                half_pairs = out.rearrange("p (n c) -> p n c", n=HALVES)[:, :, q // 2 * PAIR:(q // 2 + 1) * PAIR]
                return nc.vector.scalar_tensor_tensor(half_pairs, t_of_pairs(banks, q), LORA_SCALE, own_of(HALVES),
                                                      ALU.mult, ALU.mult)

            def lo_of_t(use, stack, t):
                dve.wait_ge(t_hi_ready, use + 1)
                lo(stack[GROUP:2 * GROUP, :], t, stack[0:GROUP, :], t_lo_ready)

            def multiply(f, banks, silu=silu, rows=P):
                dve.wait_ge(silu_done, f + 1)
                dve.wait_ge(gate_up_done, f + 1)
                up = banks[0:rows].rearrange("p n c -> p (n c)")
                nc.vector.tensor_tensor(up, silu, up, ALU.mult).then_inc(mult_done, 1)

            def lo_of_act(f, banks, rows=P):
                dve.wait_ge(act_hi_ready, f + 1)
                at = bass.ds(f, 1)
                nc.vector.tensor_tensor(act_lo[0:rows, at, :].rearrange("p a n -> p (a n)"),
                                        banks[0:rows].rearrange("p n c -> p (n c)"),
                                        act_hi[0:rows, at, :].rearrange("p a n -> p (a n)").bitcast(F32),
                                        ALU.subtract).then_inc(act_lo_ready, 1)

            def wrap_indices():
                dve.wait_ge(idx_loaded, 16)
                for t, n in ((0, ADAPTERS), (1, LABELERS)):
                    last = nc.vector.tensor_scalar(idx_wrap[:, t, :], idx_raw[:, t, :], 0, n, ALU.is_lt, ALU.mult)
                last.then_inc(idx_step, 1)
                dve.wait_ge(idx_step, 1)
                nc.vector.tensor_tensor(idx_sum[:, :, :], idx_raw[:, :, :], idx_wrap[:, :, :], ALU.add).then_inc(idx_step, 1)
                dve.wait_ge(idx_step, 2)
                for t, n in ((0, ADAPTERS), (1, LABELERS)):
                    last = nc.vector.tensor_scalar(idx[:, t, :], idx_sum[:, t, :], 0, n - 1, ALU.max, ALU.min)
                last.then_inc(idx_step, 1)

            i = 0
            for k in range(HC):
                dve.wait_ge(w_hi_ready, k + 1)
                cols = slice(k * piece, (k + 1) * piece)
                lo(w_lo[:, 0, cols], w_raw[:, 0, cols], w_hi[:, 0, cols], w_lo_ready)
                for tok in x_pieces[k]:
                    dve.wait_ge(x_hi_ready, i + 1)
                    lo(x_lo[:, k, tok], x_full[:, k, tok], x_hi[:, k, tok], x_lo_ready)
                    i += 1
                if k == 0:
                    wrap_indices()
            for g in range(2):
                for i, ((out, raw), (hi, _)) in enumerate(zip(short_parts(short_lo, g), short_parts(short_hi, g))):
                    dve.wait_ge(short_hi_ready, 3 * g + i + 1)
                    lo(out, raw, hi, short_lo_ready)
            lo_of_weights(2, 0)

            def t_of_short(g):
                dve.wait_ge(t_done, g + 1)
                values = first_banks(1)[g][SHORT:P].rearrange("p n (j c) -> p (n j) c", c=PAIR)
                nc.vector.scalar_tensor_tensor(t_full[g].rearrange("p (q c) -> p q c", c=PAIR), values, LORA_SCALE,
                                               own_of(PAIRS_OF_SEQS), ALU.mult, ALU.mult).then_inc(t_full_ready, 1)
                lo_of_t(g, t_stacks[g], t_full[g])

            dve.wait_ge(own_loaded, 16)
            dve.wait_ge(short_lo_ready, 6)
            t_of_short(0)
            t_of_short(1)
            lo_of_weights(3, 1)
            multiply(0, first_banks(0)[1])
            multiply(1, first_banks(1)[1], silu_short, SHORT)
            lo_of_act(0, first_banks(0)[1])
            lo_of_act(1, first_banks(1)[1], SHORT)

            def evacuate(f, s):
                multiply(f, up_banks(s))
                lo_of_act(f, up_banks(s))

            def step(f, s):
                lo_of_weights(f + 1, 1 - s)
                evacuate(f, s)

            evacuate(2, 0)
            with dve.Fori(1, PAIRS - 1) as pair:
                step(2 * pair + 1, 1)
                step(2 * pair + 2, 0)
            step(FC - 2, 1)
            for s in range(2):
                dve.wait_ge(a_down_hi_ready, s + 1)
                lo(a_down_parts(a_down_hl, 1, s), a_down_loaded_columns(s), a_down_parts(a_down_hl, 0, s), a_down_lo_ready)

            def lo_of_down(i, slot):
                dve.wait_ge(down_hi_ready, i + 1)
                cols = slice(slot * H, (slot + 1) * H)
                lo(w_lo[:, 1, cols], w_raw[:, 1, cols], w_hi[:, 1, cols], down_lo_ready)

            def lo_of_one(k, slot, half):
                dve.wait_ge(one_hi_ready, k + 1)
                cols = slice(half * H, (half + 1) * H)
                lo(w_lo[:, slot, cols], w_raw[:, slot, cols], w_hi[:, slot, cols], one_lo_ready)

            lo_of_down(0, 0)
            lo_of_down(1, 1)
            evacuate(FC - 1, 0)
            lo_of_one(0, 0, 0)
            lo_of_one(1, 0, 1)
            dve.wait_ge(t_done, 3)
            for q in range(2 * HALVES):
                last = t_of_group(t_down[q % 2], t_banks, q)
            last.then_inc(t_down_left, 1)
            dve.wait_ge(t_down_left, 1)
            nc.vector.tensor_tensor(t_down[0], t_down[0], t_down[1], ALU.add).then_inc(t_down_ready, 1)
            dve.wait_ge(b_down_hi_ready, 1)
            lo(down_short_lo[SHORT:P], b_down_raw, down_short_hi[SHORT:P], b_down_ready)
            dve.wait_ge(t_down_hi_ready, 1)
            lo(act_lo[SHORT:P, 1, :], t_down[0], act_hi[SHORT:P, 1, :], t_down_lo_ready)
            with dve.Fori(1, PAIRS) as pair:
                lo_of_down(2 * pair, 0)
                lo_of_down(2 * pair + 1, 1)
            dve.wait_ge(down_hi_ready, FC)
            lo(down_short_lo[0:SHORT], down_short_loaded(), down_short_hi[0:SHORT], down_lo_ready)
            for s in range(2):
                dve.wait_ge(a_one_hi_ready, s + 1)
                lo(a_one_hl[:, :, :, 1, s, :], a_one_loaded_columns(s), a_one_hl[:, :, :, 0, s, :], a_one_lo_ready)
            lo_of_one(2, 1, 1)

            def add_x(c):
                dve.wait_ge(down_done, c + 1)
                dve.wait_ge(x_full_ready, c + 1)
                at = psum[:, bank_of(c):bank_of(c) + 2, :].rearrange("p n c -> p (n c)")
                nc.vector.tensor_tensor(x_full[:, c, :], at, x_full[:, c, :], ALU.add).then_inc(x1_ready, 1)

            def lo_of_x1(c):
                dve.wait_ge(x1_hi_ready, c + 1)
                lo(x_lo[:, c, :], x_full[:, c, :], x_hi[:, c, :], x1_lo_ready)

            add_x(0)
            for c in range(1, HC):
                add_x(c)
                lo_of_x1(c - 1)
            lo_of_x1(HC - 1)
            lo_of_one(3, 1, 0)
            for s in range(2):
                dve.wait_ge(t_one_part_ready, s + 1)
                last = nc.vector.scalar_tensor_tensor(tokens_of(t_one, s), t_one_of(2 + s, s), LORA_SCALE,
                                                      tokens_of(t_one, s), ALU.mult, ALU.add)
            last.then_inc(t_full_ready, 1)
            lo_of_t(2, t_stack, t_one)
            for i, (o, tok) in enumerate(out_pieces):
                dve.wait_ge(out_done, HALVES * o + tok.start // HALF + 1)
                at = psum[:, bank_of(o) + tok.start // HALF, tok.start % HALF:(tok.stop - 1) % HALF + 1]
                nc.vector.tensor_tensor(x_full[:, o, tok], at, x_full[:, o, tok], ALU.add).then_inc(out_ready, 1)

        @block.tensor
        def _(pe):
            def product(out, w_parts, v_parts, first):
                (w_h, w_l), (v_h, v_l) = w_parts, v_parts
                for w, v in ((w_h, v_h), (w_h, v_l), (w_l, v_h)):
                    for n in range(HALVES):
                        mm = nc.tensor.matmul(out[:, n, :], w, v[:, n * HALF:(n + 1) * HALF],
                                              start=first and w is w_h and v is v_h, stop=False)
                return mm

            def t_product(k):
                for q in range(PAIRS_OF_SEQS):
                    n, j = divmod(q, 2)
                    a = a_late[:, (PAIRS_OF_SEQS * k + q) * P:(PAIRS_OF_SEQS * k + q + 1) * P]
                    for v in (x_hi, x_lo):
                        mm = nc.tensor.matmul(t_banks[:, n, j * PAIR:(j + 1) * PAIR], a, v[:, k, q * PAIR:(q + 1) * PAIR],
                                              start=k == 0 and j == 0 and v is x_hi, stop=k == HC - 1 and j == 1 and v is x_lo)
                return mm

            def adapters(out, stack_of, t):
                for q in range(PAIRS_OF_SEQS):
                    n, j = divmod(q, 2)
                    mm = nc.tensor.matmul(out[:, n, j * PAIR:(j + 1) * PAIR], stack_of(q), t[:, q * PAIR:(q + 1) * PAIR],
                                          start=False, stop=j == 1)
                return mm

            def gate_up_chunk(k, s, g, out):
                cols = slice((2 * k + g) * P, (2 * k + g + 1) * P)
                return product(out, (w_hi[:, s, cols], w_lo[:, s, cols]), (x_hi[:, k, :], x_lo[:, k, :]), k == 0)

            def gate_up_adapters(f, s, g, out, short=False):
                pe.wait_ge(b_ready, f + 1)
                if short:
                    for n in range(HALVES):
                        nc.tensor.matmul(out[SHORT:P, n, :], zeros[:, :], warm[:, :], start=True, stop=False)
                adapters(out, lambda q: b_stack[:, s, (2 * q + g) * P:(2 * q + g + 1) * P], t_stacks[g]
                         ).then_inc((gate_done, gate_up_done)[g], 1)

            def short_chunk(k, g):
                for q in range(PAIRS_OF_SEQS):
                    n, j = divmod(q, 2)
                    tok = slice(q * PAIR, (q + 1) * PAIR)
                    out = first_banks(1)[g][:, n, j * PAIR:(j + 1) * PAIR]
                    for w, v in ((short_hi, x_hi), (short_hi, x_lo), (short_lo, x_hi)):
                        mm = nc.tensor.matmul(out, w[:, k, g, q, :], v[:, k, tok],
                                              start=k == 0 and j == 0 and w is short_hi and v is x_hi, stop=False)
                    if k == HC - 1 and j == 1:
                        mm = nc.tensor.matmul(out[SHORT:P, 0:GROUP], zeros[:, :], zeros[:, :], start=False, stop=True)
                return mm

            def step(f, s):
                pe.wait_ge(w_hi_ready, PIECES + f - 1)
                pe.wait_ge(w_lo_ready, PIECES + f - 1)
                pe.wait_ge(silu_done, f - 1)
                pe.wait_ge(act_lo_ready, f - 1)
                for k in range(HC):
                    for g, out in enumerate((gate_banks(s), up_banks(s))):
                        gate_up_chunk(k, s, g, out)
                for g, out in enumerate((gate_banks(s), up_banks(s))):
                    gate_up_adapters(f, s, g, out)

            pe.wait_ge(warm_set, 1)
            for i in range(WARM_UP):
                nc.tensor.matmul(psum[:, 7, :], warm[:, 0:P], warm[:, :], start=True, stop=True)

            pe.wait_ge(w_hi_ready, 1)
            for n, tok in enumerate(x_pieces[0]):
                pe.wait_ge(x_hi_ready, n + 1)
                for w, v in ((w_hi, x_hi), (w_lo, x_hi), (w_hi, x_lo)):
                    if n == 0 and w is w_lo:
                        pe.wait_ge(w_lo_ready, 1)
                    if v is x_lo:
                        pe.wait_ge(x_lo_ready, n + 1)
                    for g, out in enumerate(first_banks(0)):
                        nc.tensor.matmul(out[:, n, :], w[:, 0, g * P:(g + 1) * P], v[:, 0, tok],
                                         start=w is w_hi and v is x_hi, stop=False)
            for k in range(1, HC):
                pe.wait_ge(w_hi_ready, k + 1)
                pe.wait_ge(w_lo_ready, k + 1)
                pe.wait_ge(x_hi_ready, X_PIECES - HC + k + 1)
                pe.wait_ge(x_lo_ready, X_PIECES - HC + k + 1)
                for g, out in enumerate(first_banks(0)):
                    mm = gate_up_chunk(k, 0, g, out)
            mm.then_inc(first_products_done, 1)
            pe.wait_ge(zeros_set, 1)
            for g in range(2):
                for k in range(HC):
                    if k == 0:
                        pe.wait_ge(short_hi_ready, 3 * (g + 1))
                        pe.wait_ge(short_lo_ready, 3 * (g + 1))
                    if g == 1 and k == HC - 1:
                        pe.wait_ge(t_again_ready, 1)
                        pe.wait_ge(t_lo_ready, 1)
                        for f in range(2):
                            gate_up_adapters(f, f, 0, first_banks(f)[0], short=f == 1)
                    mm = short_chunk(k, g)
                mm.then_inc(t_done, 1)
            pe.wait_ge(w_hi_ready, PIECES + 1)
            pe.wait_ge(w_lo_ready, PIECES + 1)
            pe.wait_ge(silu_done, 1)
            for k in range(HC):
                gate_up_chunk(k, 0, 0, gate_banks(0))
            pe.wait_ge(t_again_ready, 2)
            pe.wait_ge(t_lo_ready, 2)
            for f in range(2):
                gate_up_adapters(f, f, 1, first_banks(f)[1], short=f == 1)
            pe.wait_ge(silu_done, 2)
            for k in range(HC):
                gate_up_chunk(k, 0, 1, up_banks(0))
            for g, out in enumerate((gate_banks(0), up_banks(0))):
                gate_up_adapters(2, 0, g, out)
            step(3, 1)
            with pe.Fori(2, PAIRS) as pair:
                step(2 * pair, 0)
                step(2 * pair + 1, 1)
            step(FC - 1, 0)

            pe.wait_ge(a_down_lo_ready, 2)
            pe.wait_ge(act_lo_ready, FC - 1)
            for f in range(FC):
                if f == FC - 1:
                    pe.wait_ge(act_lo_ready, FC)
                for n in range(HALVES):
                    for v in (act_hi, act_lo):
                        mm = nc.tensor.matmul(t_banks[:, n, :],
                                              a_down_hl[0:rows_of(f), f, n * P:(n + 1) * P],
                                              v[0:rows_of(f), f, n * HALF:(n + 1) * HALF],
                                              start=f == 0 and v is act_hi, stop=f == FC - 1 and v is act_lo)
            mm.then_inc(t_done, 1)

            def banks(c):
                return psum[:, bank_of(c):bank_of(c) + 2, :]

            def down_step(i, chunk, slot, first=False):
                pe.wait_ge(down_hi_ready, i + 1)
                pe.wait_ge(down_lo_ready, i + 1)
                v_parts = [v[:, bass.ds(chunk, 1), :].rearrange("p a n -> p (a n)") for v in (act_hi, act_lo)]
                for c in range(HC):
                    if first and c == HC - 1:
                        pe.wait_ge(t_down_left, 1)
                    cols = slice(slot * H + c * P, slot * H + (c + 1) * P)
                    mm = product(banks(c), (w_hi[:, 1, cols], w_lo[:, 1, cols]), v_parts, first)
                mm.then_inc(down_step_done, 1)

            down_step(0, 0, 0, first=True)
            down_step(1, 2, 1)
            with pe.Fori(1, PAIRS) as pair:
                down_step(2 * pair, 2 * pair + 1, 0)
                down_step(2 * pair + 1, 2 * pair + 2, 1)
            pe.wait_ge(down_hi_ready, FC)
            pe.wait_ge(down_lo_ready, FC)
            pe.wait_ge(b_down_ready, 1)
            pe.wait_ge(t_down_hi_ready, 1)
            pe.wait_ge(t_down_lo_ready, 1)
            for c in range(HC):
                for q in range(PAIRS_OF_SEQS):
                    n, j = divmod(q, 2)
                    for w, v in ((down_short_hi, act_hi), (down_short_hi, act_lo), (down_short_lo, act_hi)):
                        mm = nc.tensor.matmul(banks(c)[:, n, j * PAIR:(j + 1) * PAIR], w[:, q, c * P:(c + 1) * P],
                                              v[:, 1, q * PAIR:(q + 1) * PAIR], start=False, stop=j == 1 and w is down_short_lo)
                mm.then_inc(down_done, 1)

            place = [(0, 0), (0, 1), (1, 1), (1, 0)]

            def one_chunk(k, o):
                slot, half = place[k]
                cols = slice(half * H + o * P, half * H + (o + 1) * P)
                product(banks(o), (w_hi[:, slot, cols], w_lo[:, slot, cols]), (x_hi[:, k, :], x_lo[:, k, :]), k == 0)

            pe.wait_ge(a_one_hi_ready, 2)
            pe.wait_ge(a_one_lo_ready, 2)
            for k in range(HC):
                pe.wait_ge(one_hi_ready, k + 1)
                pe.wait_ge(one_lo_ready, k + 1)
                pe.wait_ge(x1_hi_ready, k + 1)
                pe.wait_ge(x1_lo_ready, k + 1)
                if k == HC - 1:
                    t_product(k).then_inc(t_done, 1)
                for o in range(HC - 1):
                    if k == 0:
                        pe.wait_ge(x1_ready, o + 1)
                    one_chunk(k, o)
                if k == 0:
                    pe.wait_ge(x1_ready, HC)
                if k < HC - 1:
                    t_product(k)

            def last_chunk(n, ks):
                o = HC - 1
                for k in ks:
                    slot, half = place[k]
                    cols = slice(half * H + o * P, half * H + (o + 1) * P)
                    for w, v in ((w_hi, x_hi), (w_hi, x_lo), (w_lo, x_hi)):
                        nc.tensor.matmul(banks(o)[:, n, :], w[:, slot, cols], v[:, k, n * HALF:(n + 1) * HALF],
                                         start=k == 0 and w is w_hi and v is x_hi, stop=False)

            pe.wait_ge(t_full_ready, 3)
            last_chunk(0, range(HC // 2))
            pe.wait_ge(b_one_ready, 1)
            pe.wait_ge(t_lo_ready, 3)
            pe.wait_ge(t_again_ready, 3)
            for o in range(HC):
                for n in range(HALVES):
                    if o == HC - 1:
                        last_chunk(n, range(HC // 2 if n == 0 else 0, HC))
                    nc.tensor.matmul(banks(o)[:, n, :], b_one_stack[:, o * P:(o + 1) * P], t_stack[:, n * HALF:(n + 1) * HALF],
                                     start=False, stop=True).then_inc(out_done, 1)


def kernel(x, itok_B_2_6, itok_B_0_2, L0_cond_W_gate, L0_cond_W_up, L0_cond_W_down, L0_cond_A_gate, L0_cond_B_gate,
           L0_cond_A_up, L0_cond_B_up, L0_cond_A_down, L0_cond_B_down, L1_cond_W, L1_cond_lora_A, L1_cond_lora_B_w):
    import numpy as np
    import concourse.bacc as bacc
    from concourse.bass_utils import run_bass_kernel_spmd

    def in_chunks(a, axis):
        a = np.moveaxis(np.asarray(a), axis, 0)
        a = np.concatenate([a[:P + SHORT], np.zeros((P - SHORT,) + a.shape[1:], a.dtype), a[P + SHORT:]])
        return np.moveaxis(a, 0, axis)

    gate_up = np.stack([in_chunks(w, 0).reshape(FC, P, HC, P) for w in (L0_cond_W_gate, L0_cond_W_up)])
    gate_up = gate_up.transpose(1, 4, 3, 0, 2).reshape(FC, P, 2 * H)
    down = in_chunks(L0_cond_W_down, 1).T.reshape(FC, P, H)
    one = np.asarray(L1_cond_W).T
    a_gate_up = np.concatenate([np.asarray(L0_cond_A_gate)[0], np.asarray(L0_cond_A_up)[0]], 1)
    a_gate_up = a_gate_up.reshape(ADAPTERS, GROUP, HC, P).transpose(0, 3, 2, 1).reshape(ADAPTERS, P, HC * GROUP)
    a_down = in_chunks(np.asarray(L0_cond_A_down)[0], 2).reshape(ADAPTERS, RANK, FC, P).transpose(0, 3, 2, 1)
    a_down = a_down.reshape(ADAPTERS, P, FC * RANK)
    a_one = np.asarray(L1_cond_lora_A).reshape(LABELERS, HC, P, GROUP).transpose(0, 2, 1, 3).reshape(LABELERS, P, HC * GROUP)
    b_gate_up = np.stack([in_chunks(np.asarray(b)[0], 1).reshape(ADAPTERS, FC, P, RANK) for b in (L0_cond_B_gate, L0_cond_B_up)])
    b_gate_up = np.tile(b_gate_up.transpose(1, 2, 4, 0, 3).reshape(ADAPTERS, FC, RANK, 2 * P), (1, 1, 3, 1))
    b_gate_up = np.pad(b_gate_up, [(0, 0), (0, FC % 2), (0, 0), (0, 0)]).reshape(ADAPTERS, -1, 2, 3 * RANK, 2 * P)
    b_gate_up = b_gate_up.transpose(0, 1, 3, 2, 4)
    b_down = np.asarray(L0_cond_B_down)[0].transpose(0, 2, 1)
    b_one = np.tile(np.asarray(L1_cond_lora_B_w).T, (3, 1))
    own = np.tile(np.repeat(np.eye(2, dtype=np.float32), P, axis=1), (RANK, 1))

    nc = bacc.Bacc("TRN2", target_bir_lowering=False, num_devices=1)
    host = {
        "x_t": np.asarray(x).reshape(TOK, H).T,
        "sequence_indices": np.concatenate([np.asarray(itok_B_2_6), np.asarray(itok_B_0_2)]).reshape(1, 2 * SEQS),
        "own": own, "w_gate_up": gate_up, "w_down": down, "w_one": one,
        "a_gate_up": a_gate_up, "a_down": a_down, "a_one": a_one,
        "b_gate_up": b_gate_up, "b_down": b_down, "b_one": b_one,
    }
    host = {name: np.ascontiguousarray(a) for name, a in host.items()}
    aps = [nc.dram_tensor(name, a.shape, mybir.dt.from_np(a.dtype), kind="ExternalInput").ap() for name, a in host.items()]
    out_t = nc.dram_tensor("out_t", (H, TOK), F32, kind="ExternalOutput").ap()
    gated_lora_mlp_then_lora_linear(nc, *aps, out_t)
    result = run_bass_kernel_spmd(nc, [host], core_ids=[0])
    return result.results[0]["out_t"].T.reshape(SEQS, P, H)
```
